# Optimizing a Trainium2 kernel written in Bass

```python
import numpy as np
import jax
import jax.numpy as jnp

def _softmax(x, axis=-1):
    return jax.nn.softmax(x, axis=axis)

def _gelu(x):
    return jax.nn.gelu(x, approximate=True)

def _silu(x):
    return jax.nn.silu(x)

def _sigmoid(x):
    return jax.nn.sigmoid(x)

def _layernorm(x, axis=-1, eps=1e-05):
    m = jnp.mean(x, axis=axis, keepdims=True)
    v = jnp.var(x, axis=axis, keepdims=True)
    return (x - m) / jnp.sqrt(v + eps)

def _scatter_add(tgt, idx, src, axis=0):
    return tgt.at[idx].add(src)

def _segment_sum(src, seg, n):
    return jax.ops.segment_sum(src, seg, n)
kernel_name = 'mk_flamingo_gated_d1_seqx_r8_90b618'

def setup_inputs(seed: int=0):
    np.random.seed(seed)
    _w = jnp.asarray

    def _rec_inputs():
        import jax
        import jax.numpy as jnp
        _rk = jax.random.key(seed)
        x = 0.0003765 + 1 * jax.random.normal(jax.random.fold_in(_rk, 1), (8, 128, 256), jnp.float32)
        _lenS = 128 - jax.random.randint(jax.random.fold_in(_rk, 7), (8,), 0, max(1, 128 // 4) + 1, jnp.int32)
        _lenS2 = 128 - jax.random.randint(jax.random.fold_in(_rk, 8), (8,), 0, max(1, 128 // 4) + 1, jnp.int32)
        _ctx_2048P = jax.random.normal(jax.random.fold_in(_rk, 11), (8, 16, 256), jnp.float32)
        _ctx_2048c = jax.random.dirichlet(jax.random.fold_in(_rk, 511), 0.3 * jnp.ones((16,), jnp.float32), (8, 128))
        _ctx_2048t = jnp.einsum('bsk,bkd->bsd', _ctx_2048c, _ctx_2048P)
        _ctx_2048t = _ctx_2048t * jax.lax.rsqrt(jnp.mean(jnp.square(_ctx_2048t)) + 1e-12) * 0.953939
        ctx_2048 = -0.000292821 + 1.00034 * (_ctx_2048t + 0.3 * jax.random.normal(jax.random.fold_in(_rk, 611), (8, 128, 256), jnp.float32))
        _g = jax.random.normal(jax.random.fold_in(_rk, 9001), (2, 1), jnp.float32)
        _g = jnp.sign(_g) * jnp.maximum(jnp.abs(_g), 1.0) + (_g == 0) * 1.0
        g_xattn = _g[0]
        g_ffn = _g[1]
        return (x, ctx_2048, g_xattn, g_ffn)
    x, ctx_2048, g_xattn, g_ffn = _rec_inputs()

    def _L0_xattn_setup():
        import jax, jax.numpy as jnp
        import numpy as np
        key = jax.random.key(seed)
        k1, k2, k3, k4, k5 = jax.random.split(key, 5)
        B, D_MODEL, L = (2, 128, 256)
        HEAD_DIM = 8
        H = D_MODEL // HEAD_DIM
        return {'k': jax.random.normal(k1, (B, D_MODEL, L), dtype=jnp.float32), 'v': jax.random.normal(k2, (B, D_MODEL, L), dtype=jnp.float32), 'q': jax.random.normal(k3, (B, D_MODEL, L), dtype=jnp.float32), 'ssm_kernel': jax.random.normal(k4, (H, L), dtype=jnp.float32), 'D': jax.random.normal(k5, (H,), dtype=jnp.float32), 'head_dim': HEAD_DIM}
    _L0_xattn_all = _L0_xattn_setup()
    _L0_xattn_in = {k: v for k, v in _L0_xattn_all.items() if k in ('ssm_kernel', 'D')}
    del _L0_xattn_all

    def _L0_ffn_setup():
        import jax, jax.numpy as jnp
        import numpy as np
        H, I, E = (256, 512, 8)
        B, S = (2, 256)
        key = jax.random.key(seed)
        ks = jax.random.split(key, 5)
        scale = 0.02
        return {'hidden_states': jax.random.normal(ks[0], (B, S, H), dtype=jnp.float32), 'router_w': jax.random.normal(ks[1], (H, E), dtype=jnp.float32) * scale, 'gate_w': jax.random.normal(ks[2], (E, H, I), dtype=jnp.float32) * scale, 'up_w': jax.random.normal(ks[3], (E, H, I), dtype=jnp.float32) * scale, 'down_w': jax.random.normal(ks[4], (E, I, H), dtype=jnp.float32) * scale}
    _L0_ffn_all = _L0_ffn_setup()
    _L0_ffn_in = {k: v for k, v in _L0_ffn_all.items() if k in ('router_w', 'gate_w', 'up_w', 'down_w')}
    del _L0_ffn_all
    return {'x': x, 'ctx_2048': ctx_2048, 'g_xattn': g_xattn, 'g_ffn': g_ffn, 'L0_xattn_ssm_kernel': _L0_xattn_in['ssm_kernel'], 'L0_xattn_D': _L0_xattn_in['D'], 'L0_ffn_router_w': _L0_ffn_in['router_w'], 'L0_ffn_gate_w': _L0_ffn_in['gate_w'], 'L0_ffn_up_w': _L0_ffn_in['up_w'], 'L0_ffn_down_w': _L0_ffn_in['down_w']}

def reference(x, ctx_2048, g_xattn, g_ffn, L0_xattn_ssm_kernel, L0_xattn_D, L0_ffn_router_w, L0_ffn_gate_w, L0_ffn_up_w, L0_ffn_down_w):
    import jax
    import jax.numpy as jnp

    def _L0_xattn_ref(k, v, q, ssm_kernel, D, head_dim):
        import jax, jax.numpy as jnp
        import numpy as np
        B, HD, L = k.shape
        H = HD // head_dim
        fft_size = 2 * L
        k_ = k.reshape(B, H, head_dim, L)
        v_ = v.reshape(B, H, head_dim, L)
        q_ = q.reshape(B, H, head_dim, L)
        kv = jnp.einsum('bhil,bhjl->bijhl', k_, v_)
        kv_f = jnp.fft.rfft(kv, n=fft_size)
        kernel_f = jnp.fft.rfft(ssm_kernel, n=fft_size)
        y = jnp.fft.irfft(kv_f * kernel_f, n=fft_size)[..., :L]
        out = y + kv * D[None, None, None, :, None]
        out = jnp.einsum('bijhl,bhil->bjhl', out, q_)
        out = jnp.transpose(out, (0, 2, 1, 3)).reshape(B, H * head_dim, L)
        return out.astype(k.dtype)

    def _L0_ffn_ref(hidden_states, router_w, gate_w, up_w, down_w):
        import jax, jax.numpy as jnp
        import numpy as np
        H, I, E = (256, 512, 8)
        B, S = (2, 256)
        hidden_shape = hidden_states.shape
        x = hidden_states.reshape(-1, hidden_shape[-1])
        route = jax.nn.sigmoid(x @ router_w)
        max_ind = jnp.argmax(route, axis=1)
        max_prob = jnp.take_along_axis(route, max_ind[:, None], axis=1)
        out = jnp.zeros_like(x)
        num_experts = gate_w.shape[0]
        for e in range(num_experts):
            mask = (max_ind == e)[:, None]
            h = jax.nn.silu(x @ gate_w[e]) * (x @ up_w[e])
            out = out + jnp.where(mask, h @ down_w[e], 0.0)
        out = out * max_prob
        return out.reshape(hidden_shape)
    x = x + jnp.tanh(g_xattn[0]) * _L0_xattn_ref(ctx_2048, ctx_2048, _layernorm(x, axis=-1), L0_xattn_ssm_kernel, L0_xattn_D, 8)
    x = x + jnp.tanh(g_ffn[0]) * _L0_ffn_ref(_layernorm(x, axis=-1), L0_ffn_router_w, L0_ffn_gate_w, L0_ffn_up_w, L0_ffn_down_w)
    return x

_drawn_inputs = setup_inputs


def setup_inputs(seed=0):
    import zlib

    import numpy as np

    out = dict(_drawn_inputs(seed))
    spreads = {}
    factors = {'L0_ffn_router_w': 8.0, 'L0_ffn_gate_w': 8.0, 'L0_ffn_up_w': 8.0, 'L0_ffn_down_w': 8.0}
    for name, (base, spread) in spreads.items():
        noise = np.random.default_rng([zlib.crc32(name.encode()), seed]).standard_normal(out[name].shape)
        drawn = base * np.exp(spread * noise) if base else spread * noise
        out[name] = jnp.asarray(drawn.astype(out[name].dtype))
    for name, factor in factors.items():
        out[name] = (out[name] * factor).astype(out[name].dtype)
    return out
```

```python
import concourse.bass as bass
from concourse import mybir
from contextlib import ExitStack


def flamingo_gated_block(nc: bass.Bass, x, ctx, g_xattn, g_ffn, conv_kernel, conv_skip,
                         router_w, gate_w, up_w, down_w, out):
    fp32 = mybir.dt.float32
    bf16 = mybir.dt.bfloat16
    i32 = mybir.dt.int32
    ALU = mybir.AluOpType
    ACT = mybir.ActivationFunctionType
    AX = mybir.AxisListType

    P = 128
    B, C, L = x.shape
    H = conv_kernel.shape[0]
    D = C // H
    LB = L // P
    PAIRS = D * D
    NP = PAIRS * B
    E, _, F = gate_w.shape
    KD = L // P
    KF = F // P
    N = B * C
    NBLK = N // P + E - 1
    EPS = 1e-5
    TR = 4
    MEAN, RSTD, COEF, TOKEN = L, L + 1, L + 2, L + 3
    ROW = L + 4
    SKIP = 4 * N

    stack = ExitStack()
    with stack:
        def sb(name, shape, dt=fp32):
            return stack.enter_context(nc.sbuf_tensor(name, shape, dt))

        def sem(name):
            return stack.enter_context(nc.semaphore(name))

        wg = sb("wg", [P, E, KD, F])
        wu = sb("wu", [P, E, KD, F])
        wd = sb("wd", [P, E, KF, L])
        wr = sb("wr", [P, KD, E])

        xcs = sb("xcs", [P, 2, B, L])
        xs = xcs[:, 0, :, :]
        cs = xcs[:, 1, :, :]
        xb = xcs[:, :, :, :].rearrange("p a b l -> p (a b l)")[:, 0:NBLK * ROW].rearrange("p (s r) -> p s r", r=ROW)
        xb_i = xb.bitcast(i32)
        kT = sb("kT", [P, LB, H, D, B])
        qT = sb("qT", [P, LB, H, D, B])
        xn2 = kT[:, :, :, :, :].rearrange("p a h d b -> p (a h d b)").rearrange("p (b l) -> p b l", b=B)
        xnT = qT[:, :, :, :, :].rearrange("p a h d b -> p (a h d b)").rearrange("p (b k c) -> p b k c", b=B, k=KD)
        toep = sb("toep", [P, TR, L])
        ring = sb("ring", [P, (TR + 2) * LB * NP])
        kv = ring[:, 0:TR * LB * NP].rearrange("p (t a i j b) -> p t a i j b", t=TR, a=LB, i=D, j=D)
        prod = ring[:, TR * LB * NP:].rearrange("p (t a i j b) -> p t a i j b", t=2, a=LB, i=D, j=D)
        att = sb("att", [P, LB, B, C])
        qn = att[:, :, :, :].rearrange("p a b c -> p (a b c)").rearrange("p (b l) -> p b l", b=B)
        xrow = sb("xrow", [P, B, ROW])
        xrow_i = xrow[:, :, :].bitcast(i32)

        kpad = sb("kpad", [H, P + L])
        conv_k = sb("conv_k", [H, L])
        skip = sb("skip", [H, 1])
        ident = sb("ident", [P, P])
        tri = sb("tri", [P, P], bf16)
        ones = sb("ones", [P, P], bf16)
        gates = sb("gates", [P, 2])
        tanhs = sb("tanhs", [P, 2])
        padrow = sb("padrow", [P, ROW])
        padrow_i = padrow[:, :].bitcast(i32)
        stats = sb("stats", [P, 2, B, 6])
        mv = sb("mv", [P, 2, B, 2])
        std = sb("std", [P, 2, B])
        rstd = sb("rstd", [P, 2, B])

        k_thr = sb("k_thr", [P, E])
        e_score = sb("e_score", [P, E])
        s_num = sb("s_num", [P, NBLK])
        tri_e = sb("tri_e", [P, E, E])
        enz = sb("enz", [P, B, E])
        prob = sb("prob", [P, B, E])
        top = sb("top", [P, B])
        cand = sb("cand", [P, B, E])
        topc = sb("topc", [P, B])
        oh = sb("oh", [P, B, E], bf16)
        cmpb = sb("cmpb", [P, E, E])
        nblk = sb("nblk", [P, E])
        startm = sb("startm", [P, E, E])
        startb = sb("startb", [P, E])
        place = sb("place", [P, B, E])
        pos = sb("pos", [P, B], i32)
        cmps = sb("cmps", [P, NBLK, E])
        blk_expert = sb("blk_expert", [P, NBLK + 1], i32)

        cut = [0]

        def ff(n):
            cut[0] += 2 * n
            return ring[:, cut[0] - 2 * n:cut[0]].rearrange("p (t n) -> p t n", t=2)

        xn, xT, sg, hid, hT, yo = ff(L), ff(L), ff(F), ff(F), ff(F), ff(L)
        tok = sb("tok", [P, 2], i32)

        bank = [stack.enter_context(nc.psum_tensor(f"bank{i}", [P, 512], fp32)) for i in range(8)]

        kpad_dram = nc.dram_tensor("kpad_dram", [H, P + L], fp32).ap()
        rows_dram = nc.dram_tensor("rows_dram", [NBLK * P, ROW], fp32).ap()

        ctx_in = sem("ctx_in"); x_in = sem("x_in"); conv_in = sem("conv_in"); gates_in = sem("gates_in")
        wr_in = sem("wr_in"); wts_in = sem("wts_in")
        kpad_zero = sem("kpad_zero"); kpad_full = sem("kpad_full"); kpad_out = sem("kpad_out")
        toep_in = [sem(f"toep_in{i}") for i in range(TR)]
        ident_made = sem("ident_made"); ident_zero = sem("ident_zero"); consts_made = sem("consts_made")
        consts_step = sem("consts_step")
        pad_made = sem("pad_made"); pad_out = sem("pad_out")
        tanh_made = sem("tanh_made")
        ln_step = sem("ln_step"); std_made = sem("std_made"); q_made = sem("q_made")
        k_turned = sem("k_turned"); kT_made = sem("kT_made")
        q_turned = sem("q_turned"); qT_made = sem("qT_made")
        kv_made = [sem(f"kv_made{i}") for i in range(TR)]
        conv_done = [sem(f"conv_done{i}") for i in range(TR)]
        conv_read = [sem(f"conv_read{i}") for i in range(2)]
        prod_made = sem("prod_made")
        att_made = sem("att_made")
        att_turned = sem("att_turned"); x2_made = sem("x2_made"); xn2_made = sem("xn2_made")
        xn2_turned = sem("xn2_turned"); xnT_made = sem("xnT_made"); logits_done = sem("logits_done")
        enz_made = sem("enz_made"); route_step = sem("route_step"); onehot_made = sem("onehot_made")
        counts_done = sem("counts_done"); pos_made = sem("pos_made"); experts_made = sem("experts_made")
        rows_out = sem("rows_out")
        xb_in = [sem(f"xb_in{i}") for i in range(2)]
        xn_made = sem("xn_made"); xn_turned = sem("xn_turned"); xT_made = sem("xT_made")
        gate_done = sem("gate_done"); up_done = sem("up_done"); silu_made = sem("silu_made")
        hid_made = sem("hid_made"); hid_turned = sem("hid_turned"); hT_made = sem("hT_made")
        down_done = sem("down_done"); y_made = sem("y_made")
        y_out = [sem(f"y_out{i}") for i in range(2)]

        PAIRED = (NBLK - 1) // 2
        assert NBLK == 1 + 2 * PAIRED

        def backwards(ap):
            *outer, (step, n) = ap.ap
            return bass.AP(ap.tensor, ap.offset + step * (n - 1), [*outer, (-step, n)])

        block = stack.enter_context(nc.Block())

        def steps(eng, one):
            one(1, 1)
            one(2, 0)
            with eng.Fori(1, (NBLK - 3) // 2) as t:
                one(t * 2 + 1, 1)
                one(t * 2 + 2, 0)
            one(NBLK - 2, (NBLK - 2) % 2)
            one(NBLK - 1, (NBLK - 1) % 2)

        @block.sync
        def _(sp):
            sp.dma_start(cs, ctx.rearrange("b c l -> c b l")).then_inc(ctx_in, 16)
            sp.dma_start(conv_k[:, :], conv_kernel).then_inc(conv_in, 16)
            sp.dma_start(skip[:, :], conv_skip.rearrange("(h o) -> h o", o=1)).then_inc(conv_in, 16)
            sp.wait_ge(kpad_full, 2)
            sp.wait_ge(kpad_zero, 1)
            sp.dma_start(kpad_dram, kpad[:, :]).then_inc(kpad_out, 16)
            sp.wait_ge(kpad_out, 16)
            with sp.Fori(0, H // TR) as t:
                for u in range(TR):
                    sp.wait_ge(conv_done[u], t + 1)
                    sp.dma_start(toep[:, u, :], bass.AP(kpad_dram.tensor, (t * TR + u) * (P + L), [[1, P], [1, L]])
                                 ).then_inc(toep_in[u], 16)
            sp.wait_ge(rows_out, 16 * B)
            sp.dma_start(xb[:, 0, :], rows_dram[0:P, :]).then_inc(xb_in[0], 16)
            sp.dma_start(xb[:, 1:NBLK, :], rows_dram[P:, :].rearrange("(s p) r -> p s r", p=P)).then_inc(xb_in[1], 16)

        @block.gpsimd
        def _(pool):
            nc.gpsimd.memset(kpad[:, L:L + P], 0.0).then_inc(kpad_zero, 1)
            nc.gpsimd.memset(ident[:, :], 0.0).then_inc(ident_zero, 1)
            pool.wait_ge(ident_zero, 1)
            nc.gpsimd.affine_select(out=ident[:, :], in_=ident[:, :], compare_op=ALU.not_equal, fill=1.0, base=0,
                                    pattern=[[-1, P]], channel_multiplier=1).then_inc(ident_made, 1)
            nc.gpsimd.memset(padrow[:, :], 0.0).then_inc(consts_step, 1)
            nc.gpsimd.memset(tri[:, :], 1.0).then_inc(consts_step, 1)
            nc.gpsimd.memset(ones[:, :], 1.0).then_inc(consts_step, 1)
            nc.gpsimd.memset(tri_e[:, :, :], 1.0).then_inc(consts_step, 1)
            pool.wait_ge(consts_step, 4)
            nc.gpsimd.iota(padrow_i[:, TOKEN:TOKEN + 1], pattern=[[0, 1]], base=SKIP,
                           channel_multiplier=0).then_inc(pad_made, 1)
            nc.gpsimd.affine_select(out=tri[:, :], in_=tri[:, :], compare_op=ALU.is_gt, fill=0.0, base=0,
                                    pattern=[[1, P]], channel_multiplier=-1).then_inc(consts_made, 1)
            nc.gpsimd.affine_select(out=tri_e[:, :, :], in_=tri_e[:, :, :], compare_op=ALU.is_gt, fill=0.0, base=0,
                                    pattern=[[1, E], [-1, E]], channel_multiplier=0).then_inc(consts_made, 1)
            nc.gpsimd.iota(k_thr[:, :], pattern=[[P, E]], base=0, channel_multiplier=0,
                           allow_small_or_imprecise_dtypes=True).then_inc(consts_made, 1)
            nc.gpsimd.iota(e_score[:, :], pattern=[[-1, E]], base=E, channel_multiplier=0,
                           allow_small_or_imprecise_dtypes=True).then_inc(consts_made, 1)
            nc.gpsimd.iota(s_num[:, :], pattern=[[1, NBLK]], base=0, channel_multiplier=0,
                           allow_small_or_imprecise_dtypes=True).then_inc(consts_made, 1)
            nc.gpsimd.iota(xrow_i[:, :, TOKEN], pattern=[[C, B]], base=0,
                           channel_multiplier=1).then_inc(consts_made, 1)
            pool.wait_ge(pad_made, 1)
            pool.dma_start(rows_dram.rearrange("(s p) r -> p s r", p=P),
                           padrow[:, :].unsqueeze(1).to_broadcast([P, NBLK, ROW])).then_inc(pad_out, 16)

            pool.wait_ge(kT_made, 4)
            with pool.Fori(0, H // TR) as t:
                for u in range(TR):
                    h = t * TR + u
                    pool.wait_ge(conv_done[u], t + 1)
                    for a in range(LB):
                        k = kT[:, a, bass.ds(h, 1), :, :].rearrange("p o d b -> p (o d) b")
                        nc.gpsimd.tensor_tensor(kv[:, u, a], k.unsqueeze(2).to_broadcast([P, D, D, B]),
                                                k.unsqueeze(1).to_broadcast([P, D, D, B]),
                                                ALU.mult).then_inc(kv_made[u], 1)
            pool.wait_ge(pad_out, 16)
            pool.wait_ge(pos_made, 1)
            pool.wait_ge(xn2_made, B)
            for b in range(B):
                pool.indirect_dma_start(out=rows_dram, out_offset=bass.IndirectOffsetOnAxis(ap=pos[:, b:b + 1], axis=0),
                                        in_=xrow[:, b, :], in_offset=None).then_inc(rows_out, 16)

            last_token = nc.gpsimd.to_reg(N - 1)

            def send(s, par):
                pool.wait_ge(y_made, s + 1)
                pool.indirect_dma_start(out=out, out_offset=bass.IndirectOffsetOnAxis(ap=tok[:, par:par + 1], axis=0),
                                        in_=yo[:, par, :], in_offset=None, bounds_check=last_token,
                                        oob_is_err=False).then_inc(y_out[par], 16)

            for s in range(NBLK):
                send(s, s % 2)
            pool.wait_ge(y_out[0], 16 * ((NBLK + 1) // 2))
            pool.wait_ge(y_out[1], 16 * (NBLK // 2))

        @block.scalar
        def _(act):
            act.dma_start(xs, x.rearrange("b c l -> c b l")).then_inc(x_in, 16)
            act.dma_start(gates[:, 0:1], g_xattn.partition_broadcast(P)).then_inc(gates_in, 16)
            act.dma_start(gates[:, 1:2], g_ffn.partition_broadcast(P)).then_inc(gates_in, 16)
            act.dma_start(wr[:, :, :], router_w.rearrange("(p k) e -> p k e", k=KD)).then_inc(wr_in, 16)
            act.wait_ge(ln_step, 1)
            nc.scalar.activation(std[:, 0, :], std[:, 0, :], ACT.Sqrt).then_inc(std_made, 1)
            act.wait_ge(x_in, 16)
            for e in range(E):
                act.dma_start(wg[:, e], gate_w[e].rearrange("(p k) f -> p k f", k=KD)).then_inc(wts_in, 16)
                act.dma_start(wu[:, e], up_w[e].rearrange("(p k) f -> p k f", k=KD)).then_inc(wts_in, 16)
                act.dma_start(wd[:, e], down_w[e].rearrange("(p k) o -> p k o", k=KF)).then_inc(wts_in, 16)
            half = B // 2
            for src, dst, turned, made in ((0, kT, k_turned, kT_made), (4, qT, q_turned, qT_made)):
                for n in range(4):
                    a, b0 = n // 2, (n % 2) * half
                    act.wait_ge(turned, n + 1)
                    nc.scalar.activation(dst[:, a, :, :, b0:b0 + half].rearrange("p h d b -> p b (h d)"),
                                         bank[src + n][:, :].rearrange("p (b c) -> p b c", b=half),
                                         ACT.Copy).then_inc(made, 1)
            act.wait_ge(gates_in, 32)
            nc.scalar.activation(tanhs[:, :], gates[:, :], ACT.Tanh).then_inc(tanh_made, 1)
            act.wait_ge(ln_step, 2)
            nc.scalar.activation(std[:, 1, :], std[:, 1, :], ACT.Sqrt).then_inc(std_made, 1)
            for n in range(4):
                act.wait_ge(xn2_turned, n + 1)
                nc.scalar.activation(xnT[:, 2 * n:2 * n + 2].rearrange("p b k c -> p (b k c)"), bank[n][:, :],
                                     ACT.Copy).then_inc(xnT_made, 1)
            act.wait_ge(logits_done, 1)
            nc.scalar.activation(enz[:, :, :], bank[4][:, 0:B * E].rearrange("p (b e) -> p b e", b=B), ACT.Exp,
                                 scale=-1.0).then_inc(enz_made, 1)

            def copy_xT(s, par):
                act.wait_ge(xn_turned, s + 1)
                nc.scalar.activation(xT[:, par, :], bank[4][:, par * L:par * L + L], ACT.Copy).then_inc(xT_made, 1)

            def silu(s, par):
                act.wait_ge(gate_done, s + 1)
                nc.scalar.activation(sg[:, par, :], bank[par][:, :], ACT.Silu).then_inc(silu_made, 1)

            def copy_hT(s, par):
                act.wait_ge(hid_turned, s + 1)
                nc.scalar.activation(hT[:, par, :], bank[5 + par][:, :], ACT.Copy).then_inc(hT_made, 1)

            def one(s, par):
                copy_hT(s - 1, 1 - par)
                silu(s, par)
                if not (isinstance(s, int) and s == NBLK - 1):
                    copy_xT(s + 1, 1 - par)

            copy_xT(0, 0)
            silu(0, 0)
            copy_xT(1, 1)
            steps(act, one)
            copy_hT(NBLK - 1, (NBLK - 1) % 2)

        @block.vector
        def _(dve):
            for par in range(2):
                dve.sem_inc(conv_read[par], 1)
            dve.wait_ge(conv_in, 32)
            nc.vector.tensor_copy(kpad[:, 0:L - 1], backwards(conv_k[:, 1:L])).then_inc(kpad_full, 1)
            nc.vector.tensor_tensor(kpad[:, L - 1:L], conv_k[:, 0:1], skip[:, :], ALU.add).then_inc(kpad_full, 1)

            own = [0]

            def link(ins):
                own[0] += 1
                ins.then_inc(route_step, 1)
                dve.wait_ge(route_step, own[0])

            def norm(n, src, dst, made):
                for b in range(B):
                    ins = nc.vector.bn_stats(stats[:, n, b, :], src(b))
                link(ins)
                for b in range(B):
                    ins = nc.vector.bn_aggr(mv[:, n, b, :], stats[:, n, b, :])
                link(ins)
                nc.vector.tensor_scalar(std[:, n, :], mv[:, n, :, 1], EPS, None, ALU.add).then_inc(ln_step, 1)
                dve.wait_ge(std_made, n + 1)
                link(nc.vector.reciprocal(rstd[:, n, :], std[:, n, :]))
                for b in range(B):
                    nc.vector.tensor_scalar(dst(b), src(b), mv[:, n, b, 0:1], rstd[:, n, b:b + 1],
                                            ALU.subtract, ALU.mult).then_inc(made, 1)

            dve.wait_ge(x_in, 16)
            norm(0, lambda b: xs[:, b, :].rearrange("p (a l) -> p a l", a=LB),
                 lambda b: backwards(qn[:, b, :].rearrange("p (a l) -> p a l", a=LB)), q_made)

            dve.wait_ge(qT_made, 4)
            prods = [0]
            with dve.Fori(0, H // TR) as t:
                for u in range(TR):
                    h = t * TR + u
                    par = u % 2
                    dve.wait_ge(conv_done[u], t + 2)
                    for a in range(LB):
                        q = qT[:, a, bass.ds(h, 1), :, :].rearrange("p o d b -> p (o d) b")
                        y = bank[2 * par + a][:, :].rearrange("p (i j b) -> p i j b", i=D, j=D)
                        ins = nc.vector.tensor_tensor(prod[:, par, a], y, q.unsqueeze(2).to_broadcast([P, D, D, B]),
                                                      ALU.mult)
                        if a == LB - 1:
                            ins.then_inc(conv_read[par], 1)
                    dve.wait_ge(conv_read[par], t * (TR // 2) + u // 2 + 2)
                    for a in range(LB):
                        o = att[:, a, :, bass.ds(h * D, D)].rearrange("p b j -> p j b")
                        nc.vector.tensor_reduce(o, prod[:, par, a].rearrange("p i j b -> p j b i"), AX.X,
                                                ALU.add).then_inc(att_made, 1)

            dve.wait_ge(tanh_made, 1)
            for n in range(4):
                dve.wait_ge(att_turned, n + 1)
                nc.vector.scalar_tensor_tensor(
                    out=xrow[:, 2 * n:2 * n + 2, 0:L].rearrange("p b (a l) -> p b a l", a=LB),
                    in0=backwards(bank[4 + n][:, :].rearrange("p (b a l) -> p b a l", b=2, a=LB)),
                    scalar=tanhs[:, 0:1], in1=xs[:, 2 * n:2 * n + 2, :].rearrange("p b (a l) -> p b a l", a=LB),
                    op0=ALU.mult, op1=ALU.add).then_inc(x2_made, 1)
            dve.wait_ge(x2_made, 4)
            norm(1, lambda b: xrow[:, b, 0:L], lambda b: xn2[:, b, :], xn2_made)
            nc.vector.tensor_copy(xrow[:, :, MEAN], mv[:, 1, :, 0])
            nc.vector.tensor_copy(xrow[:, :, RSTD], rstd[:, 1, :])

            def over_e(ap):
                return ap.unsqueeze(2).to_broadcast([P, B, E])

            def per_b(ap):
                return ap.unsqueeze(1).to_broadcast([P, B, E])

            dve.wait_ge(enz_made, 1)
            dve.wait_ge(consts_made, 6)
            link(nc.vector.tensor_scalar(enz[:, :, :], enz[:, :, :], 1.0, None, ALU.add))
            link(nc.vector.reciprocal(prob[:, :, :], enz[:, :, :]))
            link(nc.vector.tensor_reduce(top[:, :], prob[:, :, :], AX.X, ALU.max))
            nc.vector.tensor_scalar(xrow[:, :, COEF], top[:, :], tanhs[:, 1:2], None, ALU.mult)
            link(nc.vector.tensor_tensor(cand[:, :, :], prob[:, :, :], over_e(top[:, :]), ALU.is_equal))
            link(nc.vector.tensor_tensor(cand[:, :, :], cand[:, :, :], per_b(e_score[:, :]), ALU.mult))
            link(nc.vector.tensor_reduce(topc[:, :], cand[:, :, :], AX.X, ALU.max))
            nc.vector.tensor_tensor(oh[:, :, :], cand[:, :, :], over_e(topc[:, :]),
                                    ALU.is_equal).then_inc(onehot_made, 1)
            dve.wait_ge(counts_done, 1)
            link(nc.vector.tensor_tensor(cmpb[:, :, :], bank[6][:, 0:E].unsqueeze(2).to_broadcast([P, E, E]),
                                         k_thr[:, :].unsqueeze(1).to_broadcast([P, E, E]), ALU.is_gt))
            link(nc.vector.memset(cmpb[:, :, 0], 1.0))
            link(nc.vector.tensor_reduce(nblk[:, :], cmpb[:, :, :], AX.X, ALU.add))
            link(nc.vector.tensor_tensor(startm[:, :, :], nblk[:, :].unsqueeze(1).to_broadcast([P, E, E]),
                                         tri_e[:, :, :], ALU.mult))
            link(nc.vector.tensor_reduce(startb[:, :], startm[:, :, :], AX.X, ALU.add))
            link(nc.vector.scalar_tensor_tensor(out=place[:, :, :], in0=per_b(startb[:, :]), scalar=float(P),
                                                in1=bank[5][:, 0:B * E].rearrange("p (b e) -> p b e", b=B),
                                                op0=ALU.mult, op1=ALU.add))
            link(nc.vector.tensor_tensor(place[:, :, :], place[:, :, :], oh[:, :, :], ALU.mult))
            with nc.allow_low_precision(reason="whole numbers below 2 ** 24"):
                nc.vector.tensor_reduce(pos[:, :], place[:, :, :], AX.X, ALU.add).then_inc(pos_made, 1)
            link(nc.vector.tensor_tensor(cmps[:, :, 1:E], startb[:, 1:E].unsqueeze(1).to_broadcast([P, NBLK, E - 1]),
                                         s_num[:, :].unsqueeze(2).to_broadcast([P, NBLK, E - 1]), ALU.is_le))
            with nc.allow_low_precision(reason="whole numbers below 2 ** 24"):
                nc.vector.tensor_reduce(blk_expert[:, 0:NBLK], cmps[:, :, 1:E], AX.X,
                                        ALU.add).then_inc(experts_made, 1)

            def normalise(s, par):
                nc.vector.tensor_scalar(xn[:, par, :], xb_at(s)[:, 0:L], xb_at(s)[:, MEAN:MEAN + 1],
                                        xb_at(s)[:, RSTD:RSTD + 1], ALU.subtract, ALU.mult).then_inc(xn_made, 1)

            def xb_at(s):
                return xb[:, s, :] if isinstance(s, int) else xb[:, bass.ds(s, 1), :].rearrange("p o r -> p (o r)")

            def xb_i_at(s):
                return xb_i[:, s, :] if isinstance(s, int) else xb_i[:, bass.ds(s, 1), :].rearrange("p o r -> p (o r)")

            def gated(s, par):
                dve.wait_ge(silu_made, s + 1)
                dve.wait_ge(up_done, s + 1)
                nc.vector.tensor_tensor(hid[:, par, :], sg[:, par, :], bank[2 + par][:, :],
                                        ALU.mult).then_inc(hid_made, 1)

            def combine(s, par, rounds):
                dve.wait_ge(down_done, s + 1)
                if rounds is not None:
                    dve.wait_ge(y_out[par], rounds)
                nc.vector.tensor_copy(tok[:, par:par + 1], xb_i_at(s)[:, TOKEN:TOKEN + 1])
                nc.vector.scalar_tensor_tensor(out=yo[:, par, :], in0=bank[7][:, par * L:par * L + L],
                                               scalar=xb_at(s)[:, COEF:COEF + 1], in1=xb_at(s)[:, 0:L],
                                               op0=ALU.mult, op1=ALU.add).then_inc(y_made, 1)

            def one(s, par):
                gated(s, par)
                combine(s - 1, 1 - par, None if isinstance(s, int) and s < 3 else (s - 1 - (1 - par)) * 8)
                if not (isinstance(s, int) and s >= NBLK - 2):
                    normalise(s + 2, par)

            dve.wait_ge(xb_in[0], 16)
            normalise(0, 0)
            dve.wait_ge(xb_in[1], 16)
            normalise(1, 1)
            gated(0, 0)
            normalise(2, 0)
            steps(dve, one)
            combine(NBLK - 1, (NBLK - 1) % 2, (NBLK - 1) // 2 * 16)

        @block.tensor
        def _(pe):
            half = B // 2
            for u in range(TR):
                pe.sem_inc(conv_done[u], 1)
            pe.wait_ge(ident_made, 1)
            pe.wait_ge(ctx_in, 16)
            for n in range(4):
                a, b0 = n // 2, (n % 2) * half
                for b in range(half):
                    mm = nc.tensor.transpose(bank[n][:, b * C:b * C + C], cs[:, b0 + b, a * P:a * P + P], ident[:, :])
                mm.then_inc(k_turned, 1)
            pe.wait_ge(q_made, B)
            for n in range(4):
                a, b0 = n // 2, (n % 2) * half
                for b in range(half):
                    mm = nc.tensor.transpose(bank[4 + n][:, b * C:b * C + C], qn[:, b0 + b, a * P:a * P + P],
                                             ident[:, :])
                mm.then_inc(q_turned, 1)
            pe.wait_ge(kT_made, 4)
            with pe.Fori(0, H // TR) as t:
                for u in range(TR):
                    par = u % 2
                    pe.wait_ge(toep_in[u], t * 16 + 16)
                    pe.wait_ge(kv_made[u], t * LB + LB)
                    pe.wait_ge(conv_read[par], t * (TR // 2) + u // 2 + 1)
                    cols = [kv[:, u, a].rearrange("p i j b -> p (i j b)") for a in range(LB)]
                    nc.tensor.matmul(bank[2 * par][:, :], toep[:, u, P:L], cols[0], start=True, stop=True)
                    nc.tensor.matmul(bank[2 * par + 1][:, :], toep[:, u, 0:P], cols[0], start=True, stop=False)
                    nc.tensor.matmul(bank[2 * par + 1][:, :], toep[:, u, P:L], cols[1], start=False,
                                     stop=True).then_inc(conv_done[u], 1)
            pe.wait_ge(att_made, H * LB)
            for n in range(4):
                for b in range(2):
                    for a in range(LB):
                        mm = nc.tensor.transpose(bank[4 + n][:, (b * LB + a) * P:(b * LB + a) * P + P],
                                                 att[:, a, 2 * n + b, :], ident[:, :])
                mm.then_inc(att_turned, 1)
            for n in range(4):
                pe.wait_ge(xn2_made, 2 * n + 2)
                for b in range(2):
                    for k in range(KD):
                        mm = nc.tensor.transpose(bank[n][:, (b * KD + k) * P:(b * KD + k) * P + P],
                                                 xn2[:, 2 * n + b, k::KD], ident[:, :])
                mm.then_inc(xn2_turned, 1)
            pe.wait_ge(wr_in, 16)
            for b in range(B):
                pe.wait_ge(xnT_made, b // 2 + 1)
                for k in range(KD):
                    mm = nc.tensor.matmul(bank[4][:, b * E:b * E + E], xnT[:, b, k, :], wr[:, k, :],
                                          start=(k == 0), stop=(k == KD - 1))
            mm.then_inc(logits_done, 1)
            pe.wait_ge(onehot_made, 1)
            pe.wait_ge(consts_made, 6)
            nc.tensor.matmul(bank[5][:, 0:B * E], tri[:, :], oh[:, :, :].rearrange("p b e -> p (b e)"),
                             start=True, stop=False)
            for k in range(1, B):
                nc.tensor.matmul(bank[5][:, k * E:B * E], ones[:, :],
                                 oh[:, 0:B - k, :].rearrange("p b e -> p (b e)"), start=False, stop=(k == B - 1))
            for b in range(B):
                mm = nc.tensor.matmul(bank[6][:, 0:E], ones[:, :], oh[:, b, :], start=(b == 0), stop=(b == B - 1))
            mm.then_inc(counts_done, 1)

            def turn_x(s, par):
                pe.wait_ge(xn_made, s + 1)
                for k in range(KD):
                    mm = nc.tensor.transpose(bank[4][:, par * L + k * P:par * L + k * P + P], xn[:, par, k::KD],
                                             ident[:, :])
                mm.then_inc(xn_turned, 1)

            def expert(s):
                at = blk_expert[0:1, s:s + 1] if isinstance(s, int) else blk_expert[0:1, bass.ds(s, 1)]
                return nc.tensor.value_load(at, min_val=0, max_val=E - 1)

            def gate_up(s, par):
                e = expert(s)
                pe.wait_ge(xT_made, s + 1)
                for w, base, done in ((wg, 0, gate_done), (wu, 2, up_done)):
                    for k in range(KD):
                        mm = nc.tensor.matmul(bank[base + par][:, :], xT[:, par, k * P:k * P + P],
                                              w[:, bass.ds(e, 1), k, :].rearrange("p o f -> p (o f)"),
                                              start=(k == 0), stop=(k == KD - 1))
                    mm.then_inc(done, 1)

            def turn_h(s, par):
                pe.wait_ge(hid_made, s + 1)
                for k in range(KF):
                    mm = nc.tensor.transpose(bank[5 + par][:, k * P:k * P + P], hid[:, par, k::KF], ident[:, :])
                mm.then_inc(hid_turned, 1)

            def down(s, par):
                e = expert(s)
                pe.wait_ge(hT_made, s + 1)
                pe.wait_ge(y_made, s)
                for k in range(KF):
                    mm = nc.tensor.matmul(bank[7][:, par * L:par * L + L], hT[:, par, k * P:k * P + P],
                                          wd[:, bass.ds(e, 1), k, :].rearrange("p o f -> p (o f)"),
                                          start=(k == 0), stop=(k == KF - 1))
                mm.then_inc(down_done, 1)

            def one(s, par):
                turn_h(s - 1, 1 - par)
                gate_up(s, par)
                down(s - 1, 1 - par)
                if not (isinstance(s, int) and s == NBLK - 1):
                    turn_x(s + 1, 1 - par)

            pe.wait_ge(experts_made, 1)
            turn_x(0, 0)
            pe.wait_ge(wts_in, 16 * 3 * E)
            gate_up(0, 0)
            turn_x(1, 1)
            steps(pe, one)
            turn_h(NBLK - 1, (NBLK - 1) % 2)
            down(NBLK - 1, (NBLK - 1) % 2)


_INS = ['x', 'ctx_2048', 'g_xattn', 'g_ffn', 'L0_xattn_ssm_kernel', 'L0_xattn_D', 'L0_ffn_router_w',
        'L0_ffn_gate_w', 'L0_ffn_up_w', 'L0_ffn_down_w']


def kernel(**inputs):
    import numpy as _np
    import concourse.bacc as _bacc
    from concourse import mybir as _mybir
    from concourse.bass_utils import run_bass_kernel_spmd as _run

    nc = _bacc.Bacc("TRN2", target_bir_lowering=False, num_devices=1)
    arrays, args = {}, []
    for name in _INS:
        a = _np.ascontiguousarray(inputs[name])
        arrays[f"in_{name}_dram"] = a
        args.append(nc.dram_tensor(f"in_{name}_dram", a.shape, _mybir.dt.from_np(a.dtype), kind="ExternalInput").ap())
    b, c, l = inputs['x'].shape
    args.append(nc.dram_tensor("out_dram", (b * c, l), _mybir.dt.float32, kind="ExternalOutput").ap())
    flamingo_gated_block(nc, *args)
    r = _run(nc, [arrays], core_ids=[0])
    return r.results[0]["out_dram"].reshape(b, c, l)
```

```python
import concourse.bass as bass
from concourse import mybir
from contextlib import ExitStack


def flamingo_gated_block(nc: bass.Bass, x, ctx, g_xattn, g_ffn, conv_kernel, conv_skip,
                         router_w, gate_w, up_w, down_w, out):
    fp32 = mybir.dt.float32
    bf16 = mybir.dt.bfloat16
    f16 = mybir.dt.float16
    i32 = mybir.dt.int32
    ALU = mybir.AluOpType
    ACT = mybir.ActivationFunctionType
    AX = mybir.AxisListType

    P = 128
    B, C, L = x.shape
    H = conv_kernel.shape[0]
    D = C // H
    LB = L // P
    PAIRS = D * D
    NP = PAIRS * B
    E, _, F = gate_w.shape
    KD = L // P
    KF = F // P
    N = B * C
    FULL = N // P
    NBLK = 2 * ((FULL + E) // 2)
    PAIRS_MIN, PAIRS_MAX = FULL // 2, NBLK // 2
    EPS = 1e-5
    TR = 4
    MEAN, RSTD, COEF = L, L + 1, L + 2
    ROW = L + 3
    SKIP = 4 * N

    stack = ExitStack()
    with stack:
        def sb(name, shape, dt=fp32):
            return stack.enter_context(nc.sbuf_tensor(name, shape, dt))

        def sem(name):
            return stack.enter_context(nc.semaphore(name))

        wg = sb("wg", [P, E, KD, F])
        wu = sb("wu", [P, E, KD, F])
        wd = sb("wd", [P, E, KF, L])
        wr = sb("wr", [P, KD, E])

        xcs = sb("xcs", [P, max(2 * B * L, NBLK * ROW)])
        xs = xcs[:, 0:B * L].rearrange("p (b l) -> p b l", b=B)
        cs = xcs[:, B * L:2 * B * L].rearrange("p (b l) -> p b l", b=B)
        xb = xcs[:, 0:NBLK * ROW].rearrange("p (s r) -> p s r", r=ROW)
        kT = sb("kT", [P, H, LB, D, B])
        qT = sb("qT", [P, H, LB, D, B])
        x2T = kT[:, :, :, :, :].rearrange("p h a d b -> p (h a d b)").rearrange("p (b k c) -> p b k c", b=B, k=KD)
        toep = sb("toep", [P, H, L])
        ring = sb("ring", [P, (TR + 2) * LB * NP])
        kv = ring[:, 0:TR * LB * NP].rearrange("p (t a i j b) -> p t a i j b", t=TR, a=LB, i=D, j=D)
        prod = ring[:, TR * LB * NP:].rearrange("p (t a i j b) -> p t a i j b", t=2, a=LB, i=D, j=D)
        att = sb("att", [P, LB, H, D, B])
        qn = att[:, :, :, :, :].rearrange("p a h j b -> p (a h j b)").rearrange("p (b l) -> p b l", b=B)
        xrow = sb("xrow", [P, B, ROW])
        kpad = sb("kpad", [H, P + L])
        conv_k = sb("conv_k", [H, L])
        skip = sb("skip", [H, 1])
        ident = sb("ident", [P, P])
        tri = sb("tri", [P, P], bf16)
        ones = sb("ones", [P, P], bf16)
        ones_f = sb("ones_f", [P, P])
        wrc = sb("wrc", [P, KD, E])
        gates = sb("gates", [P, 2])
        tanhs = sb("tanhs", [P, 2])
        stats = sb("stats", [P, 2, B, 6])
        mv = sb("mv", [P, 2, B, 2])
        std = sb("std", [P, 2, B])
        rstd = sb("rstd", [P, 2, B])
        shift = sb("shift", [P, B])

        k_thr = sb("k_thr", [P, FULL])
        e_score = sb("e_score", [P, E])
        s_num = sb("s_num", [P, NBLK + 1])
        row_num = sb("row_num", [P, P])
        token = sb("token", [P, B])
        odd = sb("odd", [P, PAIRS_MAX])
        tri_e = sb("tri_e", [P, E, E])
        z = sb("z", [P, B, E])
        enz = sb("enz", [P, B, E])
        prob = sb("prob", [P, B, E])
        top = sb("top", [P, B])
        cand = sb("cand", [P, B, E])
        topc = sb("topc", [P, B])
        oh = sb("oh", [P, B, E], bf16)
        cmpb = sb("cmpb", [P, E, FULL])
        nblk = sb("nblk", [P, E])
        startm = sb("startm", [P, E, E])
        startb = sb("startb", [P, E])
        place = sb("place", [P, B, E])
        rank = sb("rank", [P, B])
        over = sb("over", [P, B, FULL])
        blks = sb("blks", [P, B])
        row_in = sb("row_in", [P, B])
        blk_of = sb("blk_of", [P, B])
        at_row = sb("at_row", [P, B, P], f16)
        at_blk = sb("at_blk", [P, B, 2, NBLK], f16)
        miss = sb("miss", [P, NBLK])
        fetch = sb("fetch", [P, NBLK], i32)
        store = sb("store", [P, NBLK], i32)
        cmpp = sb("cmpp", [P, PAIRS_MAX])
        n_blk = sb("n_blk", [P, 1])
        n_last = sb("n_last", [P, 1], i32)
        cmps = sb("cmps", [P, NBLK, E])
        blk_expert = sb("blk_expert", [P, NBLK], i32)

        cut = [0]

        def ff(n):
            cut[0] += 2 * n
            return ring[:, cut[0] - 2 * n:cut[0]].rearrange("p (t n) -> p t n", t=2)

        xn, xT, sg, hid, hT, yo = ff(L), ff(L), ff(F), ff(F), ff(F), ff(L)

        banks = stack.enter_context(nc.psum_tensor("banks", [P, 8, 512], fp32))
        bank = [banks[:, i, :] for i in range(8)]

        kpad_dram = nc.dram_tensor("kpad_dram", [H, P + L], fp32).ap()
        rows_dram = nc.dram_tensor("rows_dram", [N, ROW], fp32).ap()

        ctx_in = sem("ctx_in"); x_in = sem("x_in"); conv_in = sem("conv_in"); gates_in = sem("gates_in")
        wr_in = sem("wr_in"); wts_in = sem("wts_in")
        kpad_zero = sem("kpad_zero"); kpad_full = sem("kpad_full"); kpad_out = sem("kpad_out")
        toep_in = [sem(f"toep_in{i}") for i in range(H // TR)]
        ident_made = sem("ident_made"); ident_zero = sem("ident_zero"); consts_made = sem("consts_made")
        consts_step = sem("consts_step")
        colsum_done = sem("colsum_done"); wrc_made = sem("wrc_made")
        tanh_made = sem("tanh_made")
        ln_step = sem("ln_step"); std_made = sem("std_made"); q_made = sem("q_made"); q_shift = sem("q_shift")
        k_turned = sem("k_turned"); kT_made = sem("kT_made")
        q_turned = sem("q_turned"); qT_made = sem("qT_made")
        kv_made = [sem(f"kv_made{i}") for i in range(TR)]
        conv_done = [sem(f"conv_done{i}") for i in range(TR)]
        conv_read = [sem(f"conv_read{i}") for i in range(2)]
        prod_made = sem("prod_made")
        att_made = sem("att_made")
        att_turned = sem("att_turned"); x2_made = sem("x2_made"); x2_turned = sem("x2_turned"); x2T_made = sem("x2T_made"); logits_done = sem("logits_done")
        z_made = sem("z_made"); enz_made = sem("enz_made"); route_step = sem("route_step"); onehot_made = sem("onehot_made")
        counts_done = sem("counts_done"); ranks_done = sem("ranks_done"); spots_made = sem("spots_made"); slots_done = sem("slots_done")
        slots_made = sem("slots_made"); experts_made = sem("experts_made")
        rows_made = sem("rows_made"); rows_out = sem("rows_out")
        xb_in = [sem(f"xb_in{i}") for i in range(2)]
        xn_made = sem("xn_made"); xn_turned = sem("xn_turned"); xT_made = sem("xT_made")
        gate_done = sem("gate_done"); up_done = sem("up_done"); silu_made = sem("silu_made")
        hid_made = sem("hid_made"); hid_turned = sem("hid_turned"); hT_made = sem("hT_made")
        down_done = sem("down_done"); y_made = sem("y_made")
        y_out = [sem(f"y_out{i}") for i in range(2)]

        def backwards(ap):
            *outer, (step, n) = ap.ap
            return bass.AP(ap.tensor, ap.offset + step * (n - 1), [*outer, (-step, n)])

        def in_time_blocks(ap, turned=False):
            ap = ap.rearrange("p (a l) -> p a l", a=LB)
            return backwards(ap) if turned else ap

        half = B // 2
        CONSTS = 8

        block = stack.enter_context(nc.Block())

        def steps(eng, one, finish):
            one(1, 1)
            one(2, 0)
            with eng.Fori(1, PAIRS_MIN - 1) as t:
                one(t * 2 + 1, 1)
                one(t * 2 + 2, 0)
            last_pair = eng.value_load(n_last[0:1, 0:1], min_val=PAIRS_MIN - 1, max_val=PAIRS_MAX - 1)
            with eng.Fori(PAIRS_MIN - 1, PAIRS_MAX - 1) as t:
                with eng.If(last_pair > t):
                    one(t * 2 + 1, 1)
                    one(t * 2 + 2, 0)
            finish(last_pair * 2 + 1, 1)

        @block.sync
        def _(sp):
            sp.dma_start(xs, x.rearrange("b c l -> c b l")).then_inc(x_in, 16)
            sp.dma_start(cs, ctx.rearrange("b c l -> c b l")).then_inc(ctx_in, 16)
            sp.wait_ge(kpad_full, 2)
            sp.wait_ge(kpad_zero, 1)
            sp.dma_start(kpad_dram, kpad[:, :]).then_inc(kpad_out, 16)
            sp.wait_ge(kpad_out, 16)
            for t in range(H // TR):
                sp.dma_start(toep[:, t * TR:(t + 1) * TR, :],
                             bass.AP(kpad_dram.tensor, t * TR * (P + L), [[1, P], [P + L, TR], [1, L]])
                             ).then_inc(toep_in[t], 16)
            with sp.Fori(0, E) as e:
                def of(w):
                    return w[:, bass.ds(e, 1)].rearrange("p o k n -> p (o k) n")

                def row(w, k):
                    return w[bass.ds(e, 1)].rearrange("o (p k) n -> p (o k) n", k=k)

                sp.dma_start(of(wg), row(gate_w, KD)).then_inc(wts_in, 16)
                sp.dma_start(of(wu), row(up_w, KD)).then_inc(wts_in, 16)
                sp.dma_start(of(wd), row(down_w, KF)).then_inc(wts_in, 16)
            sp.wait_ge(rows_made, 1)
            sp.dma_start(rows_dram.rearrange("(b c) r -> c b r", b=B), xrow[:, :, :]).then_inc(rows_out, 16)

        @block.gpsimd
        def _(pool):
            nc.gpsimd.memset(kpad[:, L:L + P], 0.0).then_inc(kpad_zero, 1)
            nc.gpsimd.memset(ident[:, :], 0.0).then_inc(ident_zero, 1)
            pool.wait_ge(ident_zero, 1)
            nc.gpsimd.affine_select(out=ident[:, :], in_=ident[:, :], compare_op=ALU.not_equal, fill=1.0, base=0,
                                    pattern=[[-1, P]], channel_multiplier=1).then_inc(ident_made, 1)
            nc.gpsimd.memset(ones_f[:, :], 1.0).then_inc(consts_step, 1)
            nc.gpsimd.memset(tri[:, :], 1.0).then_inc(consts_step, 1)
            nc.gpsimd.memset(ones[:, :], 1.0).then_inc(consts_step, 1)
            nc.gpsimd.memset(tri_e[:, :, :], 1.0).then_inc(consts_step, 1)
            pool.wait_ge(consts_step, 4)
            nc.gpsimd.affine_select(out=tri[:, :], in_=tri[:, :], compare_op=ALU.is_gt, fill=0.0, base=0,
                                    pattern=[[1, P]], channel_multiplier=-1).then_inc(consts_made, 1)
            nc.gpsimd.affine_select(out=tri_e[:, :, :], in_=tri_e[:, :, :], compare_op=ALU.is_gt, fill=0.0, base=0,
                                    pattern=[[1, E], [-1, E]], channel_multiplier=0).then_inc(consts_made, 1)

            def count(dst, pattern, base=0, per_partition=0):
                nc.gpsimd.iota(dst, pattern=pattern, base=base, channel_multiplier=per_partition,
                               allow_small_or_imprecise_dtypes=True).then_inc(consts_made, 1)

            count(k_thr[:, :], [[P, FULL]])
            count(e_score[:, :], [[-1, E]], base=E)
            count(s_num[:, :], [[1, NBLK + 1]])
            count(row_num[:, :], [[1, P]])
            count(token[:, :], [[C, B]], per_partition=1)
            count(odd[:, :], [[2, PAIRS_MAX]])

            pool.wait_ge(kT_made, 4)
            with pool.Fori(0, H // TR) as t:
                for u in range(TR):
                    h = t * TR + u
                    pool.wait_ge(conv_done[u], t + 1)
                    for a in range(LB):
                        k = kT[:, bass.ds(h, 1), a, :, :].rearrange("p o d b -> p (o d) b")
                        nc.gpsimd.tensor_tensor(kv[:, u, a], k.unsqueeze(2).to_broadcast([P, D, D, B]),
                                                k.unsqueeze(1).to_broadcast([P, D, D, B]),
                                                ALU.mult).then_inc(kv_made[u], 1)

            def gather(s):
                if s >= 2:
                    pool.wait_ge(xb_in[s % 2], 16 * (s // 2))
                pool.indirect_dma_start(out=xb[:, s, :], out_offset=None, in_=rows_dram,
                                        in_offset=bass.IndirectOffsetOnAxis(ap=fetch[:, s:s + 1], axis=0)
                                        ).then_inc(xb_in[s % 2], 16)

            last_token = nc.gpsimd.to_reg(N - 1)

            def send(s):
                pool.wait_ge(y_made, s + 1)
                pool.indirect_dma_start(out=out, out_offset=bass.IndirectOffsetOnAxis(ap=store[:, s:s + 1], axis=0),
                                        in_=yo[:, s % 2, :], in_offset=None, bounds_check=last_token,
                                        oob_is_err=False).then_inc(y_out[s % 2], 16)

            pool.wait_ge(slots_made, 1)
            pool.wait_ge(rows_out, 16)
            for s in range(4):
                gather(s)
            pool.wait_ge(slots_made, 3)
            pool.wait_ge(experts_made, 1)
            last_pair = pool.value_load(n_last[0:1, 0:1], min_val=PAIRS_MIN - 1, max_val=PAIRS_MAX - 1)

            def pair(one, j):
                if j < PAIRS_MIN:
                    one(2 * j)
                    one(2 * j + 1)
                elif j < PAIRS_MAX:
                    with pool.If(last_pair > j - 1):
                        one(2 * j)
                        one(2 * j + 1)

            for j in range(PAIRS_MAX):
                pair(gather, j + 2)
                pair(send, j)
            pool.wait_ge(y_out[0], last_pair * 16 + 16)
            pool.wait_ge(y_out[1], last_pair * 16 + 16)

        @block.scalar
        def _(act):
            act.dma_start(conv_k[:, :], conv_kernel).then_inc(conv_in, 16)
            act.dma_start(skip[:, :], conv_skip.rearrange("(h o) -> h o", o=1)).then_inc(conv_in, 16)
            act.dma_start(wr[:, :, :], router_w.rearrange("(p k) e -> p k e", k=KD)).then_inc(wr_in, 16)
            act.dma_start(gates[:, 0:1], g_xattn.partition_broadcast(P)).then_inc(gates_in, 16)
            act.dma_start(gates[:, 1:2], g_ffn.partition_broadcast(P)).then_inc(gates_in, 16)
            act.wait_ge(ln_step, 1)
            nc.scalar.activation(std[:, 0, :], std[:, 0, :], ACT.Sqrt).then_inc(std_made, 1)
            act.wait_ge(q_shift, 1)
            for b in range(half, B):
                nc.scalar.activation(in_time_blocks(qn[:, b, :], True), in_time_blocks(xs[:, b, :]), ACT.Identity,
                                     bias=shift[:, b:b + 1], scale=rstd[:, 0, b:b + 1]).then_inc(q_made, 1)
            for src, dst, turned, made in ((0, kT, k_turned, kT_made), (4, qT, q_turned, qT_made)):
                for n in range(4):
                    a, b0 = n // 2, (n % 2) * half
                    act.wait_ge(turned, n + 1)
                    nc.scalar.activation(dst[:, :, a, :, b0:b0 + half].rearrange("p h d b -> p b h d"),
                                         bank[src + n][:, :].rearrange("p (b h d) -> p b h d", b=half, d=D),
                                         ACT.Copy).then_inc(made, 1)
            act.wait_ge(gates_in, 32)
            nc.scalar.activation(tanhs[:, :], gates[:, :], ACT.Tanh).then_inc(tanh_made, 1)
            for n in range(4):
                act.wait_ge(x2_turned, n + 1)
                nc.scalar.activation(x2T[:, 2 * n:2 * n + 2].rearrange("p b k c -> p (b k c)"), bank[n][:, :],
                                     ACT.Copy).then_inc(x2T_made, 1)
            act.wait_ge(ln_step, 2)
            nc.scalar.activation(std[:, 1, :], std[:, 1, :], ACT.Sqrt).then_inc(std_made, 1)
            act.wait_ge(z_made, 1)
            nc.scalar.activation(enz[:, :, :], z[:, :, :], ACT.Exp, scale=-1.0).then_inc(enz_made, 1)

            def copy_xT(s, par):
                act.wait_ge(xn_turned, s + 1)
                nc.scalar.activation(xT[:, par, :], bank[4][:, par * L:par * L + L], ACT.Copy).then_inc(xT_made, 1)

            def silu(s, par):
                act.wait_ge(gate_done, s + 1)
                nc.scalar.activation(sg[:, par, :], bank[par][:, :], ACT.Silu).then_inc(silu_made, 1)

            def copy_hT(s, par):
                act.wait_ge(hid_turned, s + 1)
                nc.scalar.activation(hT[:, par, :], bank[5 + par][:, :], ACT.Copy).then_inc(hT_made, 1)

            def one(s, par):
                copy_hT(s - 1, 1 - par)
                silu(s, par)
                copy_xT(s + 1, 1 - par)

            def finish(s, par):
                copy_hT(s - 1, 1 - par)
                silu(s, par)
                copy_hT(s, par)

            copy_xT(0, 0)
            silu(0, 0)
            copy_xT(1, 1)
            act.wait_ge(experts_made, 1)
            steps(act, one, finish)

        @block.vector
        def _(dve):
            for par in range(2):
                dve.sem_inc(conv_read[par], 1)
            dve.wait_ge(conv_in, 32)
            nc.vector.tensor_copy(kpad[:, 0:L - 1], backwards(conv_k[:, 1:L])).then_inc(kpad_full, 1)
            nc.vector.tensor_tensor(kpad[:, L - 1:L], conv_k[:, 0:1], skip[:, :], ALU.add).then_inc(kpad_full, 1)

            own = [0]

            def link(ins):
                own[0] += 1
                ins.then_inc(route_step, 1)
                dve.wait_ge(route_step, own[0])

            def statistics(n):
                for b in range(B):
                    ins = nc.vector.bn_aggr(mv[:, n, b, :], stats[:, n, b, :])
                link(ins)
                nc.vector.tensor_scalar(std[:, n, :], mv[:, n, :, 1], EPS, None, ALU.add).then_inc(ln_step, 1)
                dve.wait_ge(std_made, n + 1)
                link(nc.vector.reciprocal(rstd[:, n, :], std[:, n, :]))

            dve.wait_ge(x_in, 16)
            for b in range(B):
                ins = nc.vector.bn_stats(stats[:, 0, b, :], xs[:, b, :])
            link(ins)
            statistics(0)
            nc.vector.scalar_tensor_tensor(out=shift[:, :], in0=mv[:, 0, :, 0], scalar=-1.0, in1=rstd[:, 0, :],
                                           op0=ALU.mult, op1=ALU.mult).then_inc(q_shift, 1)
            for b in range(half):
                nc.vector.tensor_scalar(in_time_blocks(qn[:, b, :], True), in_time_blocks(xs[:, b, :]),
                                        mv[:, 0, b, 0:1], rstd[:, 0, b:b + 1],
                                        ALU.subtract, ALU.mult).then_inc(q_made, 1)
            dve.wait_ge(colsum_done, 1)
            for k in range(KD):
                nc.vector.scalar_tensor_tensor(out=wrc[:, k, :], in0=bank[7][:, 0:E], scalar=-1.0 / L,
                                               in1=wr[:, k, :], op0=ALU.mult, op1=ALU.add).then_inc(wrc_made, 1)

            dve.wait_ge(qT_made, 4)
            with dve.Fori(0, H // TR) as t:
                for u in range(TR):
                    h = t * TR + u
                    par = u % 2
                    dve.wait_ge(conv_done[u], t + 2)
                    q = qT[:, bass.ds(h, 1), :, :, :].rearrange("p o a d b -> p (o a d) b")
                    y = banks[:, 2 * par:2 * par + 2, :].rearrange("p a (i j b) -> p (a i) j b", i=D, j=D)
                    nc.vector.tensor_tensor(prod[:, par].rearrange("p a i j b -> p (a i) j b"), y,
                                            q.unsqueeze(2).to_broadcast([P, LB * D, D, B]),
                                            ALU.mult).then_inc(conv_read[par], 1)
                    dve.wait_ge(conv_read[par], t * (TR // 2) + u // 2 + 2)
                    o = att[:, :, bass.ds(h, 1), :, :].rearrange("p a o j b -> p (a o) (j b)")
                    nc.vector.tensor_reduce(o, prod[:, par].rearrange("p a i j b -> p a (j b) i"), AX.X,
                                            ALU.add).then_inc(att_made, 1)

            dve.wait_ge(tanh_made, 1)
            for n in range(4):
                dve.wait_ge(att_turned, n + 1)
                nc.vector.scalar_tensor_tensor(
                    out=xrow[:, 2 * n:2 * n + 2, 0:L].rearrange("p b (a l) -> p b a l", a=LB),
                    in0=backwards(bank[4 + n][:, :].rearrange("p (b a l) -> p b a l", b=2, a=LB)),
                    scalar=tanhs[:, 0:1], in1=xs[:, 2 * n:2 * n + 2, :].rearrange("p b (a l) -> p b a l", a=LB),
                    op0=ALU.mult, op1=ALU.add).then_inc(x2_made, 1)
                dve.wait_ge(x2_made, n + 1)
                for b in (2 * n, 2 * n + 1):
                    ins = nc.vector.bn_stats(stats[:, 1, b, :], xrow[:, b, 0:L])
            link(ins)
            statistics(1)
            nc.vector.tensor_copy(xrow[:, :, MEAN], mv[:, 1, :, 0])
            nc.vector.tensor_copy(xrow[:, :, RSTD], rstd[:, 1, :])

            def over_e(ap):
                return ap.unsqueeze(2).to_broadcast([P, B, E])

            def per_b(ap):
                return ap.unsqueeze(1).to_broadcast([P, B, E])

            dve.wait_ge(logits_done, 1)
            nc.vector.tensor_tensor(z[:, :, :], bank[7][:, 0:B * E].rearrange("p (b e) -> p b e", b=B),
                                    over_e(rstd[:, 1, :]), ALU.mult).then_inc(z_made, 1)
            dve.wait_ge(enz_made, 1)
            dve.wait_ge(consts_made, CONSTS)
            link(nc.vector.tensor_scalar(enz[:, :, :], enz[:, :, :], 1.0, None, ALU.add))
            link(nc.vector.reciprocal(prob[:, :, :], enz[:, :, :]))
            link(nc.vector.tensor_reduce(top[:, :], prob[:, :, :], AX.X, ALU.max))
            nc.vector.tensor_scalar(xrow[:, :, COEF], top[:, :], tanhs[:, 1:2], None, ALU.mult).then_inc(rows_made, 1)
            link(nc.vector.tensor_tensor(cand[:, :, :], prob[:, :, :], over_e(top[:, :]), ALU.is_equal))
            link(nc.vector.tensor_tensor(cand[:, :, :], cand[:, :, :], per_b(e_score[:, :]), ALU.mult))
            link(nc.vector.tensor_reduce(topc[:, :], cand[:, :, :], AX.X, ALU.max))
            nc.vector.tensor_tensor(oh[:, :, :], cand[:, :, :], over_e(topc[:, :]),
                                    ALU.is_equal).then_inc(onehot_made, 1)
            dve.wait_ge(ranks_done, 1)
            link(nc.vector.tensor_tensor(place[:, :, :], bank[5][:, 0:B * E].rearrange("p (b e) -> p b e", b=B),
                                         oh[:, :, :], ALU.mult))
            link(nc.vector.tensor_reduce(rank[:, :], place[:, :, :], AX.X, ALU.add))
            link(nc.vector.tensor_tensor(over[:, :, :], rank[:, :].unsqueeze(2).to_broadcast([P, B, FULL]),
                                         k_thr[:, :].unsqueeze(1).to_broadcast([P, B, FULL]), ALU.is_ge))
            link(nc.vector.tensor_reduce(blks[:, :], over[:, :, 1:FULL], AX.X, ALU.add))
            link(nc.vector.scalar_tensor_tensor(out=row_in[:, :], in0=blks[:, :], scalar=-float(P), in1=rank[:, :],
                                                op0=ALU.mult, op1=ALU.add))
            nc.vector.tensor_tensor(at_row[:, :, :], row_in[:, :].unsqueeze(2).to_broadcast([P, B, P]),
                                    row_num[:, :].unsqueeze(1).to_broadcast([P, B, P]),
                                    ALU.is_equal).then_inc(spots_made, 1)
            link(nc.vector.tensor_tensor(cmpb[:, :, :], bank[6][:, 0:E].unsqueeze(2).to_broadcast([P, E, FULL]),
                                         k_thr[:, :].unsqueeze(1).to_broadcast([P, E, FULL]), ALU.is_gt))
            link(nc.vector.tensor_reduce(nblk[:, :], cmpb[:, :, :], AX.X, ALU.add))
            link(nc.vector.tensor_tensor(startm[:, :, :], nblk[:, :].unsqueeze(1).to_broadcast([P, E, E]),
                                         tri_e[:, :, :], ALU.mult))
            link(nc.vector.tensor_reduce(startb[:, :], startm[:, :, :], AX.X, ALU.add))
            link(nc.vector.tensor_tensor(place[:, :, :], per_b(startb[:, :]), oh[:, :, :], ALU.mult))
            link(nc.vector.tensor_reduce(blk_of[:, :], place[:, :, :], AX.X, ALU.add))
            link(nc.vector.tensor_tensor(blk_of[:, :], blk_of[:, :], blks[:, :], ALU.add))
            link(nc.vector.tensor_tensor(at_blk[:, :, 1, :], blk_of[:, :].unsqueeze(2).to_broadcast([P, B, NBLK]),
                                         s_num[:, 0:NBLK].unsqueeze(1).to_broadcast([P, B, NBLK]), ALU.is_equal))
            nc.vector.tensor_tensor(at_blk[:, :, 0, :], at_blk[:, :, 1, :],
                                    token[:, :].unsqueeze(2).to_broadcast([P, B, NBLK]),
                                    ALU.mult).then_inc(spots_made, 1)
            link(nc.vector.tensor_tensor(n_blk[:, :], startb[:, E - 1:E], nblk[:, E - 1:E], ALU.add))
            link(nc.vector.tensor_tensor(cmpp[:, :], n_blk[:, :].to_broadcast([P, PAIRS_MAX]), odd[:, :], ALU.is_gt))
            link(nc.vector.tensor_tensor(cmps[:, :, 1:E], startb[:, 1:E].unsqueeze(1).to_broadcast([P, NBLK, E - 1]),
                                         s_num[:, 0:NBLK].unsqueeze(2).to_broadcast([P, NBLK, E - 1]), ALU.is_le))
            with nc.allow_low_precision(reason="whole numbers below 2 ** 24"):
                nc.vector.tensor_reduce(n_last[:, :], cmpp[:, 1:PAIRS_MAX], AX.X, ALU.add)
                nc.vector.tensor_reduce(blk_expert[:, :], cmps[:, :, 1:E], AX.X, ALU.add).then_inc(experts_made, 1)
            dve.wait_ge(slots_done, 1)
            nc.vector.tensor_copy(fetch[:, :], bank[7][:, 0:NBLK]).then_inc(slots_made, 1)
            nc.vector.tensor_scalar(miss[:, :], bank[7][:, NBLK:2 * NBLK], -float(SKIP), float(SKIP),
                                    ALU.mult, ALU.add).then_inc(slots_made, 1)
            dve.wait_ge(slots_made, 2)
            nc.vector.tensor_tensor(store[:, :], miss[:, :], bank[7][:, 0:NBLK], ALU.add).then_inc(slots_made, 1)

            def xb_at(s):
                return xb[:, s, :] if isinstance(s, int) else xb[:, bass.ds(s, 1), :].rearrange("p o r -> p (o r)")

            def normalise(s, par, arrived):
                dve.wait_ge(xb_in[par], arrived)
                nc.vector.tensor_scalar(xn[:, par, :], xb_at(s)[:, 0:L], xb_at(s)[:, MEAN:MEAN + 1],
                                        xb_at(s)[:, RSTD:RSTD + 1], ALU.subtract, ALU.mult).then_inc(xn_made, 1)

            def gated(s, par):
                dve.wait_ge(silu_made, s + 1)
                dve.wait_ge(up_done, s + 1)
                nc.vector.tensor_tensor(hid[:, par, :], sg[:, par, :], bank[2 + par][:, :],
                                        ALU.mult).then_inc(hid_made, 1)

            def combine(s, par, sent):
                dve.wait_ge(down_done, s + 1)
                if sent is not None:
                    dve.wait_ge(y_out[par], sent)
                nc.vector.scalar_tensor_tensor(out=yo[:, par, :], in0=bank[7][:, par * L:par * L + L],
                                               scalar=xb_at(s)[:, COEF:COEF + 1], in1=xb_at(s)[:, 0:L],
                                               op0=ALU.mult, op1=ALU.add).then_inc(y_made, 1)

            def one(s, par):
                normalise(s + 1, 1 - par, (s + par) * 8 + 16)
                gated(s, par)
                combine(s - 1, 1 - par, None if isinstance(s, int) else (s - 1 - (1 - par)) * 8)

            def finish(s, par):
                gated(s, par)
                combine(s - 1, 1 - par, (s - 1 - (1 - par)) * 8)
                combine(s, par, (s - par) * 8)

            normalise(0, 0, 16)
            normalise(1, 1, 16)
            gated(0, 0)
            dve.wait_ge(experts_made, 1)
            steps(dve, one, finish)

        @block.tensor
        def _(pe):
            for u in range(TR):
                pe.sem_inc(conv_done[u], 1)
            pe.wait_ge(ident_made, 1)
            pe.wait_ge(ctx_in, 16)
            for n in range(4):
                a, b0 = n // 2, (n % 2) * half
                for b in range(half):
                    mm = nc.tensor.transpose(bank[n][:, b * C:b * C + C], cs[:, b0 + b, a * P:a * P + P], ident[:, :])
                mm.then_inc(k_turned, 1)
            pe.wait_ge(q_made, B)
            for n in range(4):
                a, b0 = n // 2, (n % 2) * half
                for b in range(half):
                    mm = nc.tensor.transpose(bank[4 + n][:, b * C:b * C + C], qn[:, b0 + b, a * P:a * P + P],
                                             ident[:, :])
                mm.then_inc(q_turned, 1)
            pe.wait_ge(kT_made, 4)
            for h in range(H):
                t, u, par = h // TR, h % TR, h % 2
                pe.wait_ge(toep_in[t], 16)
                pe.wait_ge(kv_made[u], (t + 1) * LB)
                pe.wait_ge(conv_read[par], h // 2 + 1)
                cols = [kv[:, u, a].rearrange("p i j b -> p (i j b)") for a in range(LB)]
                nc.tensor.matmul(bank[2 * par][:, :], toep[:, h, P:L], cols[0], start=True, stop=True)
                nc.tensor.matmul(bank[2 * par + 1][:, :], toep[:, h, 0:P], cols[0], start=True, stop=False)
                nc.tensor.matmul(bank[2 * par + 1][:, :], toep[:, h, P:L], cols[1], start=False,
                                 stop=True).then_inc(conv_done[u], 1)
                if h == 1:
                    pe.wait_ge(qT_made, 4)
                    pe.wait_ge(wr_in, 16)
                    pe.wait_ge(consts_step, 4)
                    for k in range(KD):
                        mm = nc.tensor.matmul(bank[7][:, 0:E], ones_f[:, :], wr[:, k, :], start=(k == 0),
                                              stop=(k == KD - 1))
                    mm.then_inc(colsum_done, 1)
            pe.wait_ge(att_made, H)
            pe.wait_ge(wrc_made, KD)
            for n in range(4):
                for b in range(2):
                    for a in range(LB):
                        mm = nc.tensor.transpose(bank[4 + n][:, (b * LB + a) * P:(b * LB + a) * P + P],
                                                 att[:, a, :, :, 2 * n + b].rearrange("p h j -> p (h j)"),
                                                 ident[:, :])
                mm.then_inc(att_turned, 1)
            for n in range(4):
                pe.wait_ge(x2_made, n + 1)
                for b in range(2):
                    for k in range(KD):
                        mm = nc.tensor.transpose(bank[n][:, (b * KD + k) * P:(b * KD + k) * P + P],
                                                 xrow[:, 2 * n + b, k:L:KD], ident[:, :])
                mm.then_inc(x2_turned, 1)
            pe.wait_ge(x2_made, 4)
            for b in range(B):
                pe.wait_ge(x2T_made, b // 2 + 1)
                for k in range(KD):
                    mm = nc.tensor.matmul(bank[7][:, b * E:b * E + E], x2T[:, b, k, :], wrc[:, k, :],
                                          start=(k == 0), stop=(k == KD - 1))
            mm.then_inc(logits_done, 1)
            pe.wait_ge(onehot_made, 1)
            pe.wait_ge(consts_made, CONSTS)
            nc.tensor.matmul(bank[5][:, 0:B * E], tri[:, :], oh[:, :, :].rearrange("p b e -> p (b e)"),
                             start=True, stop=False)
            for k in range(1, B):
                nc.tensor.matmul(bank[5][:, k * E:B * E], ones[:, :],
                                 oh[:, 0:B - k, :].rearrange("p b e -> p (b e)"), start=False, stop=(k == B - 1))
            for b in range(B):
                mm = nc.tensor.matmul(bank[6][:, 0:E], ones[:, :], oh[:, b, :], start=(b == 0), stop=(b == B - 1))
            mm.then_inc(ranks_done, 1)
            pe.wait_ge(spots_made, 2)
            for b in range(B):
                mm = nc.tensor.matmul(bank[7][:, 0:2 * NBLK], at_row[:, b, :],
                                      at_blk[:, b, :, :].rearrange("p a s -> p (a s)"),
                                      start=(b == 0), stop=(b == B - 1))
            mm.then_inc(slots_done, 1)

            def turn_x(s, par):
                pe.wait_ge(xn_made, s + 1)
                for k in range(KD):
                    mm = nc.tensor.transpose(bank[4][:, par * L + k * P:par * L + k * P + P], xn[:, par, k::KD],
                                             ident[:, :])
                mm.then_inc(xn_turned, 1)

            def expert(s):
                at = blk_expert[0:1, s:s + 1] if isinstance(s, int) else blk_expert[0:1, bass.ds(s, 1)]
                return nc.tensor.value_load(at, min_val=0, max_val=E - 1)

            def gate_up(s, par):
                e = expert(s)
                pe.wait_ge(xT_made, s + 1)
                for w, base, done in ((wg, 0, gate_done), (wu, 2, up_done)):
                    for k in range(KD):
                        mm = nc.tensor.matmul(bank[base + par][:, :], xT[:, par, k * P:k * P + P],
                                              w[:, bass.ds(e, 1), k, :].rearrange("p o f -> p (o f)"),
                                              start=(k == 0), stop=(k == KD - 1))
                    mm.then_inc(done, 1)

            def turn_h(s, par):
                pe.wait_ge(hid_made, s + 1)
                for k in range(KF):
                    mm = nc.tensor.transpose(bank[5 + par][:, k * P:k * P + P], hid[:, par, k::KF], ident[:, :])
                mm.then_inc(hid_turned, 1)

            def down(s, par):
                e = expert(s)
                pe.wait_ge(hT_made, s + 1)
                pe.wait_ge(y_made, s)
                for k in range(KF):
                    mm = nc.tensor.matmul(bank[7][:, par * L:par * L + L], hT[:, par, k * P:k * P + P],
                                          wd[:, bass.ds(e, 1), k, :].rearrange("p o f -> p (o f)"),
                                          start=(k == 0), stop=(k == KF - 1))
                mm.then_inc(down_done, 1)

            def one(s, par):
                turn_h(s - 1, 1 - par)
                gate_up(s, par)
                turn_x(s + 1, 1 - par)
                down(s - 1, 1 - par)

            def finish(s, par):
                turn_h(s - 1, 1 - par)
                gate_up(s, par)
                down(s - 1, 1 - par)
                turn_h(s, par)
                down(s, par)

            pe.wait_ge(experts_made, 1)
            turn_x(0, 0)
            pe.wait_ge(wts_in, 16 * 3 * E)
            gate_up(0, 0)
            turn_x(1, 1)
            steps(pe, one, finish)


_INS = ['x', 'ctx_2048', 'g_xattn', 'g_ffn', 'L0_xattn_ssm_kernel', 'L0_xattn_D', 'L0_ffn_router_w',
        'L0_ffn_gate_w', 'L0_ffn_up_w', 'L0_ffn_down_w']


def kernel(**inputs):
    import numpy as _np
    import concourse.bacc as _bacc
    from concourse import mybir as _mybir
    from concourse.bass_utils import run_bass_kernel_spmd as _run

    nc = _bacc.Bacc("TRN2", target_bir_lowering=False, num_devices=1)
    arrays, args = {}, []
    for name in _INS:
        a = _np.ascontiguousarray(inputs[name])
        arrays[f"in_{name}_dram"] = a
        args.append(nc.dram_tensor(f"in_{name}_dram", a.shape, _mybir.dt.from_np(a.dtype), kind="ExternalInput").ap())
    b, c, l = inputs['x'].shape
    args.append(nc.dram_tensor("out_dram", (b * c, l), _mybir.dt.float32, kind="ExternalOutput").ap())
    flamingo_gated_block(nc, *args)
    r = _run(nc, [arrays], core_ids=[0])
    return r.results[0]["out_dram"].reshape(b, c, l)
```

```python
import concourse.bass as bass
from concourse import mybir
from contextlib import ExitStack


def flamingo_gated_block(nc: bass.Bass, x, ctx, g_xattn, g_ffn, conv_kernel, conv_skip,
                         router_w, gate_w, up_w, down_w, out):
    fp32 = mybir.dt.float32
    bf16 = mybir.dt.bfloat16
    f16 = mybir.dt.float16
    i32 = mybir.dt.int32
    ALU = mybir.AluOpType
    ACT = mybir.ActivationFunctionType
    AX = mybir.AxisListType

    P = 128
    B, C, L = x.shape
    H = conv_kernel.shape[0]
    D = C // H
    LB = L // P
    APART = D // 2 + 1
    LEFT = D // 2 - 1
    RIGHT = D // 2
    KEPT = LEFT + D + RIGHT
    FIRSTS = LEFT + D
    NP = APART * FIRSTS * B
    DB = D * B
    assert APART + LEFT == D
    E, _, F = gate_w.shape
    KD = L // P
    KF = F // P
    N = B * C
    PIECE = KD * F
    PIECES = 3 * E
    AHEAD = H * L // PIECE
    assert KF * L == PIECE and H * L == AHEAD * PIECE
    POOL_LOWS = 10
    EARLY = 12
    WSCALE, XSCALE, HSCALE = 256.0, 16.0, 4.0
    FULL = N // P
    NBLK = FULL + E - 1
    TURNS = (NBLK - 1) // 2
    SURE = (FULL - 2) // 2
    assert FULL % 2 == 0 and NBLK == 2 * TURNS + 1
    EPS = 1e-5
    TR = 4
    MEAN, RSTD, COEF = L, L + 1, L + 2
    ROW = L + 3
    SKIP = 4 * N

    stack = ExitStack()
    with stack:
        def sb(name, shape, dt=fp32):
            return stack.enter_context(nc.sbuf_tensor(name, shape, dt))

        def sem(name):
            return stack.enter_context(nc.semaphore(name))

        store_w = sb("store_w", [P, AHEAD + PIECES, PIECE])
        parts = store_w[:, :, :].rearrange("p q n -> p (q n)").bitcast(f16).rearrange("p (q n) -> p q n", n=2 * PIECE)
        wr = sb("wr", [P, KD, E])

        xcs = sb("xcs", [P, max(2 * B * L, NBLK * ROW)])
        xs = xcs[:, 0:B * L].rearrange("p (b l) -> p b l", b=B)
        cs = xcs[:, B * L:2 * B * L].rearrange("p (b l) -> p b l", b=B)
        xb = xcs[:, 0:NBLK * ROW].rearrange("p (s r) -> p s r", r=ROW)
        kT = sb("kT", [P, H, LB, KEPT, B])
        qT = sb("qT", [P, H, LB, KEPT, B])
        x2T = kT[:, :, :, :, :].rearrange("p h a d b -> p (h a d b)")[:, 0:B * L].rearrange(
            "p (b k c) -> p b k c", b=B, k=KD)
        toep = store_w[:, 0:AHEAD, :].rearrange("p q n -> p (q n)").rearrange("p (h l) -> p h l", h=H)
        ring = sb("ring", [P, TR * LB * NP + TR * LB * D * DB])
        kv = ring[:, 0:TR * LB * NP].rearrange("p (t a n) -> p t a n", t=TR, a=LB)
        prod = ring[:, TR * LB * NP:].rearrange("p (t a i n) -> p t a i n", t=TR, a=LB, i=D)
        att = sb("att", [P, LB, H, D, B])
        qn = att[:, :, :, :, :].rearrange("p a h j b -> p (a h j b)").rearrange("p (b l) -> p b l", b=B)
        xrow = ring[:, 0:B * ROW].rearrange("p (b r) -> p b r", b=B)
        kpad = sb("kpad", [H, P + L])
        conv_k = sb("conv_k", [H, L])
        skip = sb("skip", [H, 1])
        ident = sb("ident", [P, P])
        tri = sb("tri", [P, P], bf16)
        ones = sb("ones", [P, P], bf16)
        ones_f = sb("ones_f", [P, P])
        wrc = sb("wrc", [P, KD, E])
        gates = sb("gates", [P, 2])
        spare = sb("spare", [P, 1])
        tanhs = sb("tanhs", [P, 2])
        stats = sb("stats", [P, 2, B, 6])
        mv = sb("mv", [P, 2, B, 2])
        std = sb("std", [P, 2, B])
        rstd = sb("rstd", [P, 2, B])
        shift = sb("shift", [P, B])

        k_thr = sb("k_thr", [P, NBLK + 1])
        e_score = sb("e_score", [P, E])
        row_num = sb("row_num", [P, P])
        token = sb("token", [P, B])
        turn_row = sb("turn_row", [P, 2, TURNS])
        tri_e = sb("tri_e", [P, E, E])
        z = sb("z", [P, B, E])
        enz = sb("enz", [P, B, E])
        low = sb("low", [P, B])
        top = sb("top", [P, B])
        cand = sb("cand", [P, B, E])
        topc = sb("topc", [P, B])
        oh = sb("oh", [P, B, E], bf16)
        cmpb = sb("cmpb", [P, E, FULL])
        nblk = sb("nblk", [P, E])
        startm = sb("startm", [P, E, E])
        startb = sb("startb", [P, E])
        place = sb("place", [P, B, E])
        row_of = sb("row_of", [P, B])
        over = sb("over", [P, B, NBLK + 1])
        row_in = sb("row_in", [P, B])
        blk_of = sb("blk_of", [P, B])
        at_row = sb("at_row", [P, B, P], f16)
        at_blk = sb("at_blk", [P, B, 2, NBLK], f16)
        miss = sb("miss", [P, NBLK])
        fetch = sb("fetch", [P, NBLK], i32)
        store = sb("store", [P, NBLK], i32)
        cmpp = sb("cmpp", [P, 2, TURNS])
        n_row = sb("n_row", [P, 1])
        n_more = sb("n_more", [P, 2], i32)
        cmps = sb("cmps", [P, NBLK, E])
        blk_expert = sb("blk_expert", [P, NBLK], i32)

        cut = [0]

        def ff(n):
            cut[0] += 2 * n
            return ring[:, cut[0] - 2 * n:cut[0]].rearrange("p (t n) -> p t n", t=2)

        def both(buf, n):
            return buf.rearrange("p t n -> p (t n)").bitcast(f16).rearrange("p (t a n) -> p t a n", t=2, a=2)

        xn, sg, hid, yo = ff(L), ff(F), ff(F), ff(L)
        xT, hT = both(ff(L), L), both(ff(F), F)

        banks = stack.enter_context(nc.psum_tensor("banks", [P, 8, 512], fp32))
        bank = [banks[:, i, :] for i in range(8)]

        kpad_dram = nc.dram_tensor("kpad_dram", [H, P + L], fp32).ap()
        rows_dram = nc.dram_tensor("rows_dram", [N, ROW], fp32).ap()

        ctx_in = [sem(f"ctx_in{i}") for i in range(2)]; x_in = [sem(f"x_in{i}") for i in range(2)]
        conv_in = sem("conv_in"); gates_in = sem("gates_in")
        wr_in = sem("wr_in"); wts_in = [sem(f"wts_in{i}") for i in range(4)]
        wts_scaled = sem("wts_scaled"); high_made = sem("high_made"); pool_low = sem("pool_low")
        dve_low = sem("dve_low")
        xT_low = sem("xT_low"); hT_low = sem("hT_low")
        last_turned = sem("last_turned"); last_high = sem("last_high"); last_low = sem("last_low")
        kpad_zero = sem("kpad_zero"); kpad_full = sem("kpad_full"); kpad_out = sem("kpad_out")
        toep_in = [sem(f"toep_in{i}") for i in range(H // TR)]
        ident_made = sem("ident_made"); ident_zero = sem("ident_zero"); consts_made = sem("consts_made")
        consts_step = sem("consts_step")
        colsum_done = sem("colsum_done"); wrc_made = sem("wrc_made")
        tanh_made = sem("tanh_made")
        ln_step = sem("ln_step"); std_made = sem("std_made"); q_made = sem("q_made"); q_made_act = sem("q_made_act")
        shift_made = sem("shift_made")
        k_turned = sem("k_turned"); kT_made = sem("kT_made"); kT_around = sem("kT_around"); qT_around = sem("qT_around")
        q_turned = sem("q_turned"); qT_made = sem("qT_made")
        kv_made = [sem(f"kv_made{i}") for i in range(TR)]
        conv_done = [sem(f"conv_done{i}") for i in range(TR)]
        conv_read = [sem(f"conv_read{i}") for i in range(2)]
        att_made = sem("att_made")
        att_turned = sem("att_turned"); x2_made = sem("x2_made"); x2_turned = sem("x2_turned")
        x2T_made = sem("x2T_made"); logits_done = sem("logits_done")
        z_made = sem("z_made"); enz_made = sem("enz_made"); route_step = sem("route_step")
        top_made = sem("top_made"); onehot_made = sem("onehot_made")
        ranks_done = sem("ranks_done"); spots_made = sem("spots_made"); slots_done = sem("slots_done")
        slots_made = sem("slots_made"); experts_made = sem("experts_made")
        rows_made = sem("rows_made"); rows_out = sem("rows_out")
        xb_in = [sem(f"xb_in{i}") for i in range(2)]
        xn_made = sem("xn_made"); xn_turned = sem("xn_turned"); xT_made = sem("xT_made")
        gate_done = sem("gate_done"); up_done = sem("up_done"); silu_made = sem("silu_made")
        hid_made = sem("hid_made"); hid_turned = sem("hid_turned"); hT_made = sem("hT_made")
        down_done = sem("down_done"); y_made = sem("y_made")
        y_out = [sem(f"y_out{i}") for i in range(2)]

        def backwards(ap):
            *outer, (step, n) = ap.ap
            return bass.AP(ap.tensor, ap.offset + step * (n - 1), [*outer, (-step, n)])

        def strided(ap, skip, dims):
            return bass.AP(ap.tensor, ap.offset + skip, [ap.ap[0], *[list(d) for d in dims]])

        def in_time_blocks(ap, turned=False):
            ap = ap.rearrange("p (a l) -> p a l", a=LB)
            return backwards(ap) if turned else ap

        def last_bank(par, i):
            return bank[5 + (par + i) % 2]

        def whole(q):
            if isinstance(q, int):
                return store_w[:, AHEAD + q, :]
            return store_w[:, bass.ds(q + AHEAD, 1), :].rearrange("p o n -> p (o n)")

        def part(q, low):
            if isinstance(q, int):
                return parts[:, q, low * PIECE:(low + 1) * PIECE]
            return parts[:, bass.ds(q, 1), low * PIECE:(low + 1) * PIECE].rearrange("p o n -> p (o n)")

        half = B // 2
        HIGH_FIRST = 8
        Q_DVE = 5
        CONSTS = 8

        block = stack.enter_context(nc.Block())

        def steps(eng, one, finish):
            evens = eng.value_load(n_more[0:1, 0:1], min_val=SURE, max_val=TURNS)
            odds = eng.value_load(n_more[0:1, 1:2], min_val=SURE, max_val=TURNS - 1)

            def on_from(s):
                if s < NBLK - 1:
                    with eng.If((odds if s % 2 == 0 else evens) > (s - 1) // 2):
                        one(s, s % 2)
                        on_from(s + 1)

            for s in range(1, 2 * SURE + 1):
                one(s, s % 2, EARLY + 2 * s < PIECES)
            on_from(2 * SURE + 1)
            with eng.If(evens > odds):
                finish(odds * 2 + 2, 0)
            with eng.If(odds > evens - 1):
                finish(odds * 2 + 1, 1)

        @block.sync
        def _(sp):
            sp.dma_start(conv_k[:, :], conv_kernel).then_inc(conv_in, 16)
            sp.dma_start(skip[:, :], conv_skip.rearrange("(h o) -> h o", o=1)).then_inc(conv_in, 16)
            for i in range(2):
                sp.dma_start(cs[:, i * half:(i + 1) * half],
                             ctx.rearrange("b c l -> c b l")[:, i * half:(i + 1) * half]).then_inc(ctx_in[i], 16)
            sp.wait_ge(kpad_full, 2)
            sp.wait_ge(kpad_zero, 1)
            sp.dma_start(kpad_dram, kpad[:, :]).then_inc(kpad_out, 16)
            for i in range(2):
                sp.dma_start(xs[:, i * half:(i + 1) * half], x.rearrange("b c l -> c b l")[:, i * half:(i + 1) * half]
                             ).then_inc(x_in[i], 16)
            sp.wait_ge(kpad_out, 16)
            for t in range(H // TR):
                sp.dma_start(toep[:, t * TR:(t + 1) * TR, :],
                             bass.AP(kpad_dram.tensor, t * TR * (P + L), [[1, P], [P + L, TR], [1, L]])
                             ).then_inc(toep_in[t], 16)

            def weights_in(w, what, e, k, arrived):
                sp.dma_start(store_w[:, bass.ds(e * 3 + (AHEAD + what), 1), :].rearrange("p o n -> p (o n)"),
                             w[bass.ds(e, 1)].rearrange("o (p k) n -> p (o k n)", k=k)).then_inc(arrived, 16)

            for g in range(4):
                with sp.Fori(g * E // 4, (g + 1) * E // 4) as e:
                    weights_in(gate_w, 0, e, KD, wts_in[g])
                    weights_in(up_w, 1, e, KD, wts_in[g])
                    weights_in(down_w, 2, e, KF, wts_in[g])
            sp.wait_ge(rows_made, 1)
            sp.dma_start(rows_dram.rearrange("(b c) r -> c b r", b=B), xrow[:, :, :]).then_inc(rows_out, 16)

        @block.gpsimd
        def _(pool):
            nc.gpsimd.memset(kpad[:, L:L + P], 0.0).then_inc(kpad_zero, 1)
            nc.gpsimd.memset(ident[:, :], 0.0).then_inc(ident_zero, 1)
            pool.wait_ge(ident_zero, 1)
            nc.gpsimd.affine_select(out=ident[:, :], in_=ident[:, :], compare_op=ALU.not_equal, fill=1.0, base=0,
                                    pattern=[[-1, P]], channel_multiplier=1).then_inc(ident_made, 1)
            nc.gpsimd.memset(ones_f[:, :], 1.0).then_inc(consts_step, 1)
            nc.gpsimd.memset(tri[:, :], 1.0).then_inc(consts_step, 1)
            nc.gpsimd.memset(ones[:, :], 1.0).then_inc(consts_step, 1)
            nc.gpsimd.memset(tri_e[:, :, :], float(P)).then_inc(consts_step, 1)
            pool.wait_ge(consts_step, 4)
            nc.gpsimd.affine_select(out=tri[:, :], in_=tri[:, :], compare_op=ALU.is_gt, fill=0.0, base=0,
                                    pattern=[[1, P]], channel_multiplier=-1).then_inc(consts_made, 1)
            nc.gpsimd.affine_select(out=tri_e[:, :, :], in_=tri_e[:, :, :], compare_op=ALU.is_gt, fill=0.0, base=0,
                                    pattern=[[1, E], [-1, E]], channel_multiplier=0).then_inc(consts_made, 1)

            def count(dst, pattern, base=0, per_partition=0):
                nc.gpsimd.iota(dst, pattern=pattern, base=base, channel_multiplier=per_partition,
                               allow_small_or_imprecise_dtypes=True).then_inc(consts_made, 1)

            count(k_thr[:, :], [[P, NBLK + 1]])
            pool.wait_ge(consts_made, 3)
            nc.gpsimd.memset(k_thr[:, 0:1], -1.0).then_inc(consts_made, 1)
            count(e_score[:, :], [[-1, E]], base=E)
            count(row_num[:, :], [[1, P]])
            count(token[:, :], [[C, B]], per_partition=1)
            count(turn_row[:, :, :], [[P, 2], [2 * P, TURNS]], base=2 * P)

            pool.wait_ge(kT_around, 8)
            with pool.Fori(0, H // TR) as t:
                for u in range(TR):
                    h = t * TR + u
                    pool.wait_ge(conv_done[u], t + 1)
                    for a in range(LB):
                        k = kT[:, bass.ds(h, 1), a, :, :].rearrange("p o d b -> p (o d b)")
                        nc.gpsimd.tensor_tensor(kv[:, u, a].rearrange("p (r n) -> p r n", r=APART),
                                                strided(k, 0, [(0, APART), (1, FIRSTS * B)]),
                                                strided(k, 0, [(B, APART), (1, FIRSTS * B)]),
                                                ALU.mult).then_inc(kv_made[u], 1)

            for q in range(POOL_LOWS):
                pool.wait_ge(high_made, q + 1)
                nc.gpsimd.tensor_tensor(part(q, 1), whole(q), part(q, 0), ALU.subtract).then_inc(pool_low, 1)

            def gather(s):
                if s >= 2:
                    pool.wait_ge(xb_in[s % 2], 16 * (s // 2))
                pool.indirect_dma_start(out=xb[:, s, :], out_offset=None, in_=rows_dram,
                                        in_offset=bass.IndirectOffsetOnAxis(ap=fetch[:, s:s + 1], axis=0)
                                        ).then_inc(xb_in[s % 2], 16)

            last_token = nc.gpsimd.to_reg(N - 1)

            def send(s):
                pool.wait_ge(y_made, s + 1)
                pool.indirect_dma_start(out=out, out_offset=bass.IndirectOffsetOnAxis(ap=store[:, s:s + 1], axis=0),
                                        in_=yo[:, s % 2, :], in_offset=None, bounds_check=last_token,
                                        oob_is_err=False).then_inc(y_out[s % 2], 16)

            pool.wait_ge(slots_made, 1)
            pool.wait_ge(rows_out, 16)
            for s in range(4):
                gather(s)
            pool.wait_ge(slots_made, 3)
            pool.wait_ge(experts_made, 1)
            more = [pool.value_load(n_more[0:1, 0:1], min_val=SURE, max_val=TURNS),
                    pool.value_load(n_more[0:1, 1:2], min_val=SURE, max_val=TURNS - 1)]

            def if_there(one, s):
                if s < FULL:
                    one(s)
                elif s < NBLK:
                    with pool.If(more[s % 2] > s // 2 - 1):
                        one(s)

            for s in range(NBLK):
                if_there(gather, s + 4)
                if_there(send, s)
            pool.wait_ge(y_out[0], more[0] * 16 + 16)
            pool.wait_ge(y_out[1], more[1] * 16 + 16)

        @block.scalar
        def _(act):
            act.dma_start(wr[:, :, :], router_w.rearrange("(p k) e -> p k e", k=KD)).then_inc(wr_in, 16)
            act.dma_start(gates[:, 0:1], g_xattn.partition_broadcast(P)).then_inc(gates_in, 16)
            act.dma_start(gates[:, 1:2], g_ffn.partition_broadcast(P)).then_inc(gates_in, 16)
            def copy_turned(src, dst, turned, made):
                for i, n in enumerate((0, 2, 1, 3)):
                    a, b0 = n // 2, (n % 2) * half
                    act.wait_ge(turned, i + 1)
                    nc.scalar.activation(dst[:, :, a, LEFT:LEFT + D, b0:b0 + half].rearrange("p h d b -> p b h d"),
                                         bank[src + n][:, :].rearrange("p (b h d) -> p b h d", b=half, d=D),
                                         ACT.Copy).then_inc(made, 1)

            def root(n):
                act.wait_ge(ln_step, n + 1)
                nc.scalar.activation(std[:, n, :], std[:, n, :], ACT.Sqrt).then_inc(std_made, 1)

            copy_turned(0, kT, k_turned, kT_made)
            root(0)
            act.wait_ge(shift_made, 1)
            for b in range(Q_DVE, B):
                nc.scalar.activation(in_time_blocks(qn[:, b, :], True), in_time_blocks(xs[:, b, :]), ACT.Identity,
                                     scale=rstd[:, 0, b:b + 1], bias=shift[:, b:b + 1]).then_inc(q_made_act, 1)
            copy_turned(4, qT, q_turned, qT_made)
            act.wait_ge(gates_in, 32)
            nc.scalar.activation(tanhs[:, :], gates[:, :], ACT.Tanh).then_inc(tanh_made, 1)
            nc.scalar.activation(spare[:, :], std[:, 0, 0:1], ACT.Sqrt)

            def high(q):
                act.wait_ge(wts_scaled, q + 1)
                if q < AHEAD:
                    act.wait_ge(conv_done[TR - 1], q + 2)
                elif q < AHEAD + POOL_LOWS:
                    act.wait_ge(pool_low, q - AHEAD + 1)
                else:
                    act.wait_ge(dve_low, q - AHEAD - POOL_LOWS + 1)
                nc.scalar.activation(part(q, 0), whole(q), ACT.Copy).then_inc(high_made, 1)

            def scale_weights(g):
                act.wait_ge(wts_in[g], 16 * PIECES // 4)
                with act.Fori(g * PIECES // 4, (g + 1) * PIECES // 4) as q:
                    nc.scalar.activation(whole(q), whole(q), ACT.Copy, scale=WSCALE).then_inc(wts_scaled, 1)

            for g in range(3):
                scale_weights(g)
                high(g)
            for q in range(3, HIGH_FIRST):
                high(q)
            for n in range(4):
                act.wait_ge(x2_turned, n + 1)
                nc.scalar.activation(x2T[:, 2 * n:2 * n + 2].rearrange("p b k c -> p (b k c)"), bank[n][:, :],
                                     ACT.Copy).then_inc(x2T_made, 1)
            high(HIGH_FIRST)
            root(1)
            act.wait_ge(z_made, 1)
            nc.scalar.activation(enz[:, :, :], z[:, :, :], ACT.Exp, scale=-1.0).then_inc(enz_made, 1)

            for q in range(HIGH_FIRST + 1, EARLY + 2):
                high(q)
            scale_weights(3)

            def copy_xT(s, par):
                act.wait_ge(xn_turned, s + 1)
                nc.scalar.activation(xT[:, par, 0, :], bank[4][:, par * L:par * L + L], ACT.Copy,
                                     scale=XSCALE).then_inc(xT_made, 1)

            def silu(s, par):
                act.wait_ge(gate_done, s + 1)
                nc.scalar.activation(sg[:, par, :], bank[par][:, :], ACT.Silu,
                                     scale=1.0 / (WSCALE * XSCALE)).then_inc(silu_made, 1)

            def copy_hT(s, par):
                act.wait_ge(hid_turned, s + 1)
                nc.scalar.activation(hT[:, par, 0, :], bank[5 + par][:, :], ACT.Copy,
                                     scale=HSCALE).then_inc(hT_made, 1)

            def one(s, par, split=False):
                copy_hT(s - 1, 1 - par)
                if split:
                    high(s * 2 + EARLY)
                silu(s, par)
                if split:
                    high(s * 2 + EARLY + 1)
                copy_xT(s + 1, 1 - par)

            def finish(s, par):
                copy_hT(s - 1, 1 - par)
                silu(s, par)
                for i in range(2):
                    act.wait_ge(last_turned, i + 1)
                    nc.scalar.activation(hT[:, par, 0, i * F // 2:(i + 1) * F // 2],
                                         last_bank(par, i)[:, i * F // 2:(i + 1) * F // 2], ACT.Copy,
                                         scale=HSCALE).then_inc(last_high, 1)

            copy_xT(0, 0)
            silu(0, 0)
            copy_xT(1, 1)
            act.wait_ge(experts_made, 1)
            steps(act, one, finish)

        @block.vector
        def _(dve):
            for par in range(2):
                dve.sem_inc(conv_read[par], 1)
            dve.wait_ge(conv_in, 32)
            nc.vector.tensor_copy(kpad[:, 0:L - 1], backwards(conv_k[:, 1:L])).then_inc(kpad_full, 1)
            nc.vector.tensor_tensor(kpad[:, L - 1:L], conv_k[:, 0:1], skip[:, :], ALU.add).then_inc(kpad_full, 1)

            own = [0]

            def link(ins, meanwhile=None):
                own[0] += 1
                ins.then_inc(route_step, 1)
                if meanwhile:
                    meanwhile()
                dve.wait_ge(route_step, own[0])

            def around(dst, made, around_made, i):
                n = (0, 2, 1, 3)[i]
                a, b0 = n // 2, (n % 2) * half
                dve.wait_ge(made, i + 1)
                for to, start, channels in ((0, D, LEFT), (LEFT + D, LEFT, RIGHT)):
                    nc.vector.tensor_copy(dst[:, :, a, to:to + channels, b0:b0 + half],
                                          dst[:, :, a, start:start + channels, b0:b0 + half]).then_inc(around_made, 1)

            def statistics(n, rows):
                for b in range(B):
                    if n == 0 and b % half == 0:
                        around(kT, kT_made, kT_around, b // 2)
                        around(kT, kT_made, kT_around, b // 2 + 1)
                        dve.wait_ge(x_in[b // half], 16)
                    ins = nc.vector.bn_stats(stats[:, n, b, :], rows[:, b, 0:L])
                link(ins)
                for b in range(B):
                    ins = nc.vector.bn_aggr(mv[:, n, b, :], stats[:, n, b, :])
                link(ins)
                nc.vector.tensor_scalar(std[:, n, :], mv[:, n, :, 1], EPS, None, ALU.add).then_inc(ln_step, 1)
                dve.wait_ge(std_made, n + 1)
                link(nc.vector.reciprocal(rstd[:, n, :], std[:, n, :]))

            statistics(0, xs)
            nc.vector.scalar_tensor_tensor(out=shift[:, :], in0=mv[:, 0, :, 0], scalar=-1.0, in1=rstd[:, 0, :],
                                           op0=ALU.mult, op1=ALU.mult).then_inc(shift_made, 1)
            for b in range(Q_DVE):
                nc.vector.tensor_scalar(in_time_blocks(qn[:, b, :], True), in_time_blocks(xs[:, b, :]),
                                        mv[:, 0, b, 0:1], rstd[:, 0, b:b + 1],
                                        ALU.subtract, ALU.mult).then_inc(q_made, 1)
            dve.wait_ge(colsum_done, 1)
            for k in range(KD):
                nc.vector.scalar_tensor_tensor(out=wrc[:, k, :], in0=bank[3][:, 0:E], scalar=-1.0 / L,
                                               in1=wr[:, k, :], op0=ALU.mult, op1=ALU.add).then_inc(wrc_made, 1)

            for i in range(4):
                around(qT, qT_made, qT_around, i)
            dve.wait_ge(qT_around, 8)
            Q, Y, FB = KEPT * B, 512, FIRSTS * B

            def multiply(h, t, u):
                par = u % 2
                dve.wait_ge(conv_done[u], t + 2)
                q = qT[:, bass.ds(h, 1), :, :, :].rearrange("p o a d b -> p (o a d b)")
                y = banks[:, 2 * par:2 * par + 2, :]
                nc.vector.tensor_tensor(prod[:, u, :, 0:APART, :],
                                        strided(y, LEFT * B, [(Y, LB), (FB, APART), (1, DB)]),
                                        strided(q, LEFT * B, [(Q, LB), (B, APART), (1, DB)]), ALU.mult)
                nc.vector.tensor_tensor(prod[:, u, :, APART:D, :],
                                        strided(y, LEFT * FB, [(Y, LB), (B - FB, LEFT), (1, DB)]),
                                        strided(q, 0, [(Q, LB), (B, LEFT), (1, DB)]),
                                        ALU.mult).then_inc(conv_read[par], 1)

            def reduce(h, t, u):
                dve.wait_ge(conv_read[u % 2], t * (TR // 2) + u // 2 + 2)
                o = att[:, :, bass.ds(h, 1), :, :].rearrange("p a o j b -> p (a o) (j b)")
                nc.vector.tensor_reduce(o, prod[:, u].rearrange("p a i n -> p a n i"), AX.X,
                                        ALU.add).then_inc(att_made, 1)

            multiply(0, 0, 0)
            with dve.Fori(0, H // TR - 1) as t:
                for u in range(TR):
                    multiply(t * TR + u + 1, t + (u + 1) // TR, (u + 1) % TR)
                    reduce(t * TR + u, t, u)
            for h in range(H - TR, H):
                if h + 1 < H:
                    multiply(h + 1, (h + 1) // TR, (h + 1) % TR)
                reduce(h, h // TR, h % TR)

            dve.wait_ge(tanh_made, 1)
            for n in range(4):
                dve.wait_ge(att_turned, n + 1)
                nc.vector.scalar_tensor_tensor(
                    out=xrow[:, 2 * n:2 * n + 2, 0:L].rearrange("p b (a l) -> p b a l", a=LB),
                    in0=backwards(bank[4 + n % 3][:, :].rearrange("p (b a l) -> p b a l", b=2, a=LB)),
                    scalar=tanhs[:, 0:1], in1=xs[:, 2 * n:2 * n + 2, :].rearrange("p b (a l) -> p b a l", a=LB),
                    op0=ALU.mult, op1=ALU.add).then_inc(x2_made, 1)
            dve.wait_ge(x2_made, 4)
            statistics(1, xrow)
            nc.vector.tensor_copy(xrow[:, :, MEAN], mv[:, 1, :, 0])
            nc.vector.tensor_copy(xrow[:, :, RSTD], rstd[:, 1, :])

            def over_e(ap):
                return ap.unsqueeze(2).to_broadcast([P, B, E])

            def per_b(ap):
                return ap.unsqueeze(1).to_broadcast([P, B, E])

            dve.wait_ge(logits_done, 4)
            nc.vector.tensor_tensor(z[:, :, :], bank[7][:, 0:B * E].rearrange("p (b e) -> p b e", b=B),
                                    over_e(rstd[:, 1, :]), ALU.mult).then_inc(z_made, 1)
            dve.wait_ge(enz_made, 1)
            dve.wait_ge(consts_made, CONSTS)
            link(nc.vector.tensor_scalar(enz[:, :, :], enz[:, :, :], 1.0, None, ALU.add))
            link(nc.vector.tensor_reduce(low[:, :], enz[:, :, :], AX.X, ALU.min))
            link(nc.vector.tensor_tensor(cand[:, :, :], enz[:, :, :], over_e(low[:, :]), ALU.is_equal))
            link(nc.vector.tensor_tensor(cand[:, :, :], cand[:, :, :], per_b(e_score[:, :]), ALU.mult),
                 lambda: nc.vector.reciprocal(top[:, :], low[:, :]).then_inc(top_made, 1))
            link(nc.vector.tensor_reduce(topc[:, :], cand[:, :, :], AX.X, ALU.max))
            nc.vector.tensor_tensor(oh[:, :, :], cand[:, :, :], over_e(topc[:, :]),
                                    ALU.is_equal).then_inc(onehot_made, 1)
            dve.wait_ge(top_made, 1)
            nc.vector.tensor_scalar(xrow[:, :, COEF], top[:, :], tanhs[:, 1:2], 1.0 / (WSCALE * HSCALE),
                                    ALU.mult, ALU.mult).then_inc(rows_made, 1)
            dve.wait_ge(ranks_done, 1)
            link(nc.vector.tensor_tensor(cmpb[:, :, :], bank[6][:, 0:E].unsqueeze(2).to_broadcast([P, E, FULL]),
                                         k_thr[:, 0:FULL].unsqueeze(1).to_broadcast([P, E, FULL]), ALU.is_gt))
            link(nc.vector.tensor_reduce(nblk[:, :], cmpb[:, :, :], AX.X, ALU.add))
            link(nc.vector.tensor_tensor(startm[:, :, :], nblk[:, :].unsqueeze(1).to_broadcast([P, E, E]),
                                         tri_e[:, :, :], ALU.mult))
            link(nc.vector.tensor_reduce(startb[:, :], startm[:, :, :], AX.X, ALU.add))
            link(nc.vector.tensor_tensor(place[:, :, :], bank[5][:, 0:B * E].rearrange("p (b e) -> p b e", b=B),
                                         per_b(startb[:, :]), ALU.add))
            link(nc.vector.tensor_tensor(place[:, :, :], place[:, :, :], oh[:, :, :], ALU.mult))
            link(nc.vector.tensor_reduce(row_of[:, :], place[:, :, :], AX.X, ALU.add))
            link(nc.vector.tensor_tensor(over[:, :, :], row_of[:, :].unsqueeze(2).to_broadcast([P, B, NBLK + 1]),
                                         k_thr[:, :].unsqueeze(1).to_broadcast([P, B, NBLK + 1]), ALU.is_ge))
            link(nc.vector.tensor_reduce(blk_of[:, :], over[:, :, 1:NBLK], AX.X, ALU.add))
            link(nc.vector.scalar_tensor_tensor(out=row_in[:, :], in0=blk_of[:, :], scalar=-float(P), in1=row_of[:, :],
                                                op0=ALU.mult, op1=ALU.add))
            nc.vector.tensor_tensor(at_blk[:, :, 1, :], over[:, :, 0:NBLK], over[:, :, 1:NBLK + 1],
                                    ALU.subtract).then_inc(spots_made, 1)
            nc.vector.tensor_tensor(at_row[:, :, :], row_in[:, :].unsqueeze(2).to_broadcast([P, B, P]),
                                    row_num[:, :].unsqueeze(1).to_broadcast([P, B, P]),
                                    ALU.is_equal).then_inc(spots_made, 1)
            dve.wait_ge(spots_made, 1)
            nc.vector.tensor_tensor(at_blk[:, :, 0, :], at_blk[:, :, 1, :],
                                    token[:, :].unsqueeze(2).to_broadcast([P, B, NBLK]),
                                    ALU.mult).then_inc(spots_made, 1)
            link(nc.vector.scalar_tensor_tensor(out=n_row[:, :], in0=nblk[:, E - 1:E], scalar=float(P),
                                                in1=startb[:, E - 1:E], op0=ALU.mult, op1=ALU.add))
            nc.vector.tensor_tensor(cmpp[:, :, :], n_row[:, :].unsqueeze(2).to_broadcast([P, 2, TURNS]),
                                    turn_row[:, :, :], ALU.is_gt)
            link(nc.vector.tensor_tensor(cmps[:, :, 1:E], startb[:, 1:E].unsqueeze(1).to_broadcast([P, NBLK, E - 1]),
                                         k_thr[:, 0:NBLK].unsqueeze(2).to_broadcast([P, NBLK, E - 1]), ALU.is_le))
            dve.wait_ge(slots_done, 1)
            nc.vector.tensor_copy(fetch[:, :], bank[7][:, 0:NBLK]).then_inc(slots_made, 1)
            nc.vector.tensor_scalar(miss[:, :], bank[7][:, NBLK:2 * NBLK], -float(SKIP), float(SKIP),
                                    ALU.mult, ALU.add).then_inc(slots_made, 1)
            with nc.allow_low_precision(reason="whole numbers below 2 ** 24"):
                nc.vector.tensor_reduce(n_more[:, :], cmpp[:, :, :], AX.X, ALU.add)
                nc.vector.tensor_reduce(blk_expert[:, :], cmps[:, :, 1:E], AX.X, ALU.add).then_inc(experts_made, 1)
            dve.wait_ge(slots_made, 2)
            nc.vector.tensor_tensor(store[:, :], miss[:, :], bank[7][:, 0:NBLK], ALU.add).then_inc(slots_made, 1)

            def xb_at(s):
                return xb[:, s, :] if isinstance(s, int) else xb[:, bass.ds(s, 1), :].rearrange("p o r -> p (o r)")

            def normalise(s, par, arrived):
                dve.wait_ge(xb_in[par], arrived)
                nc.vector.tensor_scalar(xn[:, par, :], xb_at(s)[:, 0:L], xb_at(s)[:, MEAN:MEAN + 1],
                                        xb_at(s)[:, RSTD:RSTD + 1], ALU.subtract, ALU.mult).then_inc(xn_made, 1)

            def split_low(q):
                dve.wait_ge(high_made, q + 1)
                nc.vector.tensor_tensor(part(q, 1), whole(q), part(q, 0), ALU.subtract).then_inc(dve_low, 1)

            def low_xT(s, par):
                dve.wait_ge(xT_made, s + 1)
                nc.vector.scalar_tensor_tensor(out=xT[:, par, 1, :], in0=bank[4][:, par * L:par * L + L],
                                               scalar=XSCALE, in1=xT[:, par, 0, :],
                                               op0=ALU.mult, op1=ALU.subtract).then_inc(xT_low, 1)

            def low_hT(s, par):
                dve.wait_ge(hT_made, s + 1)
                nc.vector.scalar_tensor_tensor(out=hT[:, par, 1, :], in0=bank[5 + par][:, :], scalar=HSCALE,
                                               in1=hT[:, par, 0, :],
                                               op0=ALU.mult, op1=ALU.subtract).then_inc(hT_low, 1)

            def gated(s, par):
                dve.wait_ge(silu_made, s + 1)
                dve.wait_ge(up_done, s + 1)
                nc.vector.scalar_tensor_tensor(out=hid[:, par, :], in0=bank[2 + par][:, :],
                                               scalar=1.0 / (WSCALE * XSCALE), in1=sg[:, par, :],
                                               op0=ALU.mult, op1=ALU.mult).then_inc(hid_made, 1)

            def combine(s, par, sent):
                dve.wait_ge(down_done, s + 1)
                if sent is not None:
                    dve.wait_ge(y_out[par], sent)
                nc.vector.scalar_tensor_tensor(out=yo[:, par, :], in0=bank[7][:, par * L:par * L + L],
                                               scalar=xb_at(s)[:, COEF:COEF + 1], in1=xb_at(s)[:, 0:L],
                                               op0=ALU.mult, op1=ALU.add).then_inc(y_made, 1)

            def one(s, par, split=False):
                low_hT(s - 1, 1 - par)
                normalise(s + 1, 1 - par, (s + par) * 8 + 16)
                if split:
                    split_low(s * 2 + EARLY)
                gated(s, par)
                low_xT(s + 1, 1 - par)
                if split:
                    split_low(s * 2 + EARLY + 1)
                combine(s - 1, 1 - par, None if isinstance(s, int) and s < 3 else (s - 1 - (1 - par)) * 8)

            def finish(s, par):
                low_hT(s - 1, 1 - par)
                gated(s, par)
                combine(s - 1, 1 - par, (s - 1 - (1 - par)) * 8)
                for i in range(2):
                    dve.wait_ge(last_high, i + 1)
                    nc.vector.scalar_tensor_tensor(out=hT[:, par, 1, i * F // 2:(i + 1) * F // 2],
                                                   in0=last_bank(par, i)[:, i * F // 2:(i + 1) * F // 2],
                                                   scalar=HSCALE,
                                                   in1=hT[:, par, 0, i * F // 2:(i + 1) * F // 2],
                                                   op0=ALU.mult, op1=ALU.subtract).then_inc(last_low, 1)
                combine(s, par, (s - par) * 8)

            for q in range(POOL_LOWS, EARLY):
                split_low(q)
            normalise(0, 0, 16)
            low_xT(0, 0)
            normalise(1, 1, 16)
            split_low(EARLY)
            gated(0, 0)
            low_xT(1, 1)
            split_low(EARLY + 1)
            dve.wait_ge(experts_made, 1)
            steps(dve, one, finish)

        @block.tensor
        def _(pe):
            some_q = qT[:, :, :, :, :].rearrange("p h a d b -> p (h a d b)")[:, 0:512].rearrange(
                "p (a l) -> p a l", a=2)

            def keep_busy(n, data, into=0):
                for _ in range(n):
                    nc.tensor.matmul(bank[into][:, :], ident[:, :], data.rearrange("p a l -> p (a l)"),
                                     start=True, stop=True)

            for u in range(TR):
                pe.sem_inc(conv_done[u], 1)
            pe.wait_ge(ident_made, 1)
            for n in (0, 2, 1, 3):
                a, b0 = n // 2, (n % 2) * half
                pe.wait_ge(ctx_in[n % 2], 16)
                for b in range(half):
                    mm = nc.tensor.transpose(bank[n][:, b * C:b * C + C], cs[:, b0 + b, a * P:a * P + P], ident[:, :])
                mm.then_inc(k_turned, 1)
            pe.wait_ge(kT_made, 4)
            pe.wait_ge(wr_in, 16)
            pe.wait_ge(consts_step, 4)
            for k in range(KD):
                mm = nc.tensor.matmul(bank[3][:, 0:E], ones_f[:, :], wr[:, k, :], start=(k == 0), stop=(k == KD - 1))
            mm.then_inc(colsum_done, 1)
            def convolve(h):
                t, u, par = h // TR, h % TR, h % 2
                pe.wait_ge(toep_in[t], 16)
                pe.wait_ge(kv_made[u], (t + 1) * LB)
                pe.wait_ge(conv_read[par], h // 2 + 1)
                if h == 1:
                    pe.wait_ge(wrc_made, KD)
                cols = [kv[:, u, a, LEFT * B:NP] for a in range(LB)]
                nc.tensor.matmul(bank[2 * par][:, LEFT * B:NP], toep[:, h, P:L], cols[0], start=True, stop=True)
                nc.tensor.matmul(bank[2 * par + 1][:, LEFT * B:NP], toep[:, h, 0:P], cols[0], start=True, stop=False)
                nc.tensor.matmul(bank[2 * par + 1][:, LEFT * B:NP], toep[:, h, P:L], cols[1], start=False,
                                 stop=True).then_inc(conv_done[u], 1)

            keep_busy(3, cs[:, 0:2])
            convolve(0)
            for n in (0, 2, 1, 3):
                a, b0 = n // 2, (n % 2) * half
                pe.wait_ge(q_made, min(b0 + half, Q_DVE))
                if b0 + half > Q_DVE:
                    pe.wait_ge(q_made_act, b0 + half - Q_DVE)
                for b in range(half):
                    mm = nc.tensor.transpose(bank[4 + n][:, b * C:b * C + C], qn[:, b0 + b, a * P:a * P + P],
                                             ident[:, :])
                mm.then_inc(q_turned, 1)
            for h in range(1, H):
                convolve(h)
            keep_busy(5, some_q, into=7)
            pe.wait_ge(att_made, H)
            for n in range(4):
                if n == 3:
                    pe.wait_ge(x2_made, 1)
                for b in range(2):
                    for a in range(LB):
                        mm = nc.tensor.transpose(bank[4 + n % 3][:, (b * LB + a) * P:(b * LB + a) * P + P],
                                                 att[:, a, :, :, 2 * n + b].rearrange("p h j -> p (h j)"),
                                                 ident[:, :])
                mm.then_inc(att_turned, 1)
            def turn_x2(n):
                pe.wait_ge(x2_made, n + 1)
                for b in range(2):
                    for k in range(KD):
                        mm = nc.tensor.transpose(bank[n][:, (b * KD + k) * P:(b * KD + k) * P + P],
                                                 xrow[:, 2 * n + b, k:L:KD], ident[:, :])
                mm.then_inc(x2_turned, 1)

            def logits(n):
                pe.wait_ge(x2T_made, n + 1)
                for b in (2 * n, 2 * n + 1):
                    for k in range(KD):
                        mm = nc.tensor.matmul(bank[7][:, b * E:b * E + E], x2T[:, b, k, :], wrc[:, k, :],
                                              start=(k == 0), stop=(k == KD - 1))
                mm.then_inc(logits_done, 1)

            turn_x2(0)
            for n in range(1, 4):
                turn_x2(n)
                logits(n - 1)
            logits(3)
            keep_busy(1, some_q)
            pe.wait_ge(onehot_made, 1)
            pe.wait_ge(consts_made, CONSTS)
            nc.tensor.matmul(bank[5][:, 0:B * E], tri[:, :], oh[:, :, :].rearrange("p b e -> p (b e)"),
                             start=True, stop=False)
            for k in range(1, B):
                nc.tensor.matmul(bank[5][:, k * E:B * E], ones[:, :],
                                 oh[:, 0:B - k, :].rearrange("p b e -> p (b e)"), start=False, stop=(k == B - 1))
            for b in range(B):
                mm = nc.tensor.matmul(bank[6][:, 0:E], ones[:, :], oh[:, b, :], start=(b == 0), stop=(b == B - 1))
            mm.then_inc(ranks_done, 1)
            keep_busy(3, some_q)
            pe.wait_ge(spots_made, 3)
            for b in range(B):
                mm = nc.tensor.matmul(bank[7][:, 0:2 * NBLK], at_row[:, b, :],
                                      at_blk[:, b, :, :].rearrange("p a s -> p (a s)"),
                                      start=(b == 0), stop=(b == B - 1))
            mm.then_inc(slots_done, 1)
            keep_busy(4, some_q)

            def turn_x(s, par):
                pe.wait_ge(xn_made, s + 1)
                for k in range(KD):
                    mm = nc.tensor.transpose(bank[4][:, par * L + k * P:par * L + k * P + P], xn[:, par, k::KD],
                                             ident[:, :])
                mm.then_inc(xn_turned, 1)

            def expert(s):
                at = blk_expert[0:1, s:s + 1] if isinstance(s, int) else blk_expert[0:1, bass.ds(s, 1)]
                return nc.tensor.value_load(at, min_val=0, max_val=E - 1)

            def product(out, x_parts, base, chunks, width, ready=lambda k: None):
                mm, first = None, True
                for k in range(chunks):
                    ready(k)
                    for x_low, w_low in ((0, 0), (0, 1), (1, 0)):
                        w = parts[:, bass.ds(base, 1), w_low * PIECE + k * width:w_low * PIECE + (k + 1) * width]
                        mm = nc.tensor.matmul(out, x_parts[:, x_low, k * P:k * P + P],
                                              w.rearrange("p o n -> p (o n)"), start=first,
                                              stop=(k == chunks - 1 and x_low == 1))
                        first = False
                return mm

            def gate_up(s, par):
                e = expert(s)
                if isinstance(s, int) and s < 3:
                    pe.wait_ge(pool_low, 3 * s + 3)
                else:
                    pe.wait_ge(pool_low, POOL_LOWS)
                    pe.wait_ge(dve_low, (min(s * 3 + 3, PIECES) if isinstance(s, int) else PIECES) - POOL_LOWS)
                pe.wait_ge(xT_low, s + 1)
                product(bank[par][:, :], xT[:, par], e * 3, KD, F).then_inc(gate_done, 1)
                product(bank[2 + par][:, :], xT[:, par], e * 3 + 1, KD, F).then_inc(up_done, 1)

            def turn_h(s, par):
                pe.wait_ge(hid_made, s + 1)
                for k in range(KF):
                    mm = nc.tensor.transpose(bank[5 + par][:, k * P:k * P + P], hid[:, par, k::KF], ident[:, :])
                mm.then_inc(hid_turned, 1)

            def turn_last_h(s, par):
                pe.wait_ge(hid_made, s + 1)
                for k in range(KF):
                    mm = nc.tensor.transpose(last_bank(par, 2 * k // KF)[:, k * P:k * P + P], hid[:, par, k::KF],
                                             ident[:, :])
                    if (k + 1) % (KF // 2) == 0:
                        mm.then_inc(last_turned, 1)

            def down(s, par, last=False):
                def half_ready(k):
                    if last and k % (KF // 2) == 0:
                        pe.wait_ge(last_low, k // (KF // 2) + 1)

                e = expert(s)
                if not last:
                    pe.wait_ge(hT_low, s + 1)
                pe.wait_ge(y_made, s)
                product(bank[7][:, par * L:par * L + L], hT[:, par], e * 3 + 2, KF, L,
                        half_ready).then_inc(down_done, 1)

            def one(s, par, split=False):
                turn_h(s - 1, 1 - par)
                gate_up(s, par)
                turn_x(s + 1, 1 - par)
                down(s - 1, 1 - par)

            def finish(s, par):
                turn_h(s - 1, 1 - par)
                gate_up(s, par)
                down(s - 1, 1 - par)
                turn_last_h(s, par)
                down(s, par, last=True)

            pe.wait_ge(experts_made, 1)
            turn_x(0, 0)
            gate_up(0, 0)
            turn_x(1, 1)
            steps(pe, one, finish)


_INS = ['x', 'ctx_2048', 'g_xattn', 'g_ffn', 'L0_xattn_ssm_kernel', 'L0_xattn_D', 'L0_ffn_router_w',
        'L0_ffn_gate_w', 'L0_ffn_up_w', 'L0_ffn_down_w']


def kernel(**inputs):
    import numpy as _np
    import concourse.bacc as _bacc
    from concourse import mybir as _mybir
    from concourse.bass_utils import run_bass_kernel_spmd as _run

    nc = _bacc.Bacc("TRN2", target_bir_lowering=False, num_devices=1)
    arrays, args = {}, []
    for name in _INS:
        a = _np.ascontiguousarray(inputs[name])
        arrays[f"in_{name}_dram"] = a
        args.append(nc.dram_tensor(f"in_{name}_dram", a.shape, _mybir.dt.from_np(a.dtype), kind="ExternalInput").ap())
    b, c, l = inputs['x'].shape
    args.append(nc.dram_tensor("out_dram", (b * c, l), _mybir.dt.float32, kind="ExternalOutput").ap())
    flamingo_gated_block(nc, *args)
    r = _run(nc, [arrays], core_ids=[0])
    return r.results[0]["out_dram"].reshape(b, c, l)
```
